# Optimizing a Trainium2 kernel written in Bass

```python
import numpy as np
import jax
import jax.numpy as jnp

def _softmax(x, axis=-1):
    return jax.nn.softmax(x, axis=axis)

def _gelu(x):
    return jax.nn.gelu(x, approximate=True)

def _silu(x):
    return jax.nn.silu(x)

def _sigmoid(x):
    return jax.nn.sigmoid(x)

def _layernorm(x, axis=-1, eps=1e-05):
    m = jnp.mean(x, axis=axis, keepdims=True)
    v = jnp.var(x, axis=axis, keepdims=True)
    return (x - m) / jnp.sqrt(v + eps)

def _scatter_add(tgt, idx, src, axis=0):
    return tgt.at[idx].add(src)

def _segment_sum(src, seg, n):
    return jax.ops.segment_sum(src, seg, n)
kernel_name = 'mk_conv_seq_d4_conv_nchw256_r4_f172ab'

def setup_inputs(seed: int=0):
    np.random.seed(seed)
    _w = jnp.asarray

    def _rec_inputs():
        import jax
        import jax.numpy as jnp
        _gk = jax.random.key(seed)
        x = 7.22e-05 + 1 * jax.random.normal(jax.random.fold_in(_gk, 1), (8, 64, 16, 16), jnp.float32)
        return x
    x = _rec_inputs()

    def _L0_conv_setup():
        import jax, jax.numpy as jnp
        import numpy as np
        key = jax.random.key(seed)
        ks = jax.random.split(key, 6)
        B, C, W, H = (8, 64, 16, 16)
        Cq, Cv = (C // 8, C // 2)
        x = jax.random.normal(ks[0], (B, C, W, H), dtype=jnp.float32)
        Wq = jax.random.normal(ks[1], (Cq, C), dtype=jnp.float32) / np.sqrt(C)
        Wk = jax.random.normal(ks[2], (Cq, C), dtype=jnp.float32) / np.sqrt(C)
        Wv = jax.random.normal(ks[3], (Cv, C), dtype=jnp.float32) / np.sqrt(C)
        Wo = jax.random.normal(ks[4], (C, Cv), dtype=jnp.float32) / np.sqrt(Cv)
        gamma = jax.random.normal(ks[5], (1,), dtype=jnp.float32) * 0.1
        return {'x': x, 'Wq': Wq, 'bq': jnp.zeros((Cq,), jnp.float32), 'Wk': Wk, 'bk': jnp.zeros((Cq,), jnp.float32), 'Wv': Wv, 'bv': jnp.zeros((Cv,), jnp.float32), 'Wo': Wo, 'bo': jnp.zeros((C,), jnp.float32), 'gamma': gamma}
    _L0_conv_all = _L0_conv_setup()
    _L0_conv_in = {k: v for k, v in _L0_conv_all.items() if k in ('Wq', 'bq', 'Wk', 'bk', 'Wv', 'bv', 'Wo', 'bo', 'gamma')}
    del _L0_conv_all

    def _L1_conv_setup():
        import jax, jax.numpy as jnp
        import numpy as np
        TEMPERATURE = 1.0
        key = jax.random.key(seed)
        ks = jax.random.split(key, 7)
        B, C, H, W = (4, 64, 16, 16)
        Cqk = C // 8
        s = 0.02
        return {'x': jax.random.normal(ks[0], (B, C, H, W), dtype=jnp.float32), 'Wq': jax.random.normal(ks[1], (Cqk, C), dtype=jnp.float32) * s, 'bq': jax.random.normal(ks[2], (Cqk,), dtype=jnp.float32) * s, 'Wk': jax.random.normal(ks[3], (Cqk, C), dtype=jnp.float32) * s, 'bk': jax.random.normal(ks[4], (Cqk,), dtype=jnp.float32) * s, 'Wv': jax.random.normal(ks[5], (C, C), dtype=jnp.float32) * s, 'bv': jax.random.normal(ks[6], (C,), dtype=jnp.float32) * s}
    _L1_conv_all = _L1_conv_setup()
    _L1_conv_in = {k: v for k, v in _L1_conv_all.items() if k in ('Wq', 'bq', 'Wk', 'bk', 'Wv', 'bv')}
    del _L1_conv_all

    def _L2_conv_setup():
        import jax, jax.numpy as jnp
        import numpy as np
        EPS = 1e-05

        def batch_norm(x, gamma, beta):
            mean = jnp.mean(x, axis=(0, 2, 3), keepdims=True)
            var = jnp.mean((x - mean) ** 2, axis=(0, 2, 3), keepdims=True)
            xhat = (x - mean) * jax.lax.rsqrt(var + EPS)
            return xhat * gamma[None, :, None, None] + beta[None, :, None, None]

        def quantize_w1bit(w):
            E = jax.lax.stop_gradient(jnp.mean(jnp.abs(w)))
            wq = E * jnp.sign(w)
            return w + jax.lax.stop_gradient(wq - w)

        def conv3x3(x, w):
            return jax.lax.conv_general_dilated(x, w, window_strides=(1, 1), padding=((1, 1), (1, 1)), dimension_numbers=('NCHW', 'OIHW', 'NCHW'))
        key = jax.random.key(seed)
        ks = jax.random.split(key, 3)
        B, Cin, Cout, H, W = (32, 64, 64, 56, 56)
        return {'x': jax.random.normal(ks[0], (B, Cin, H, W), jnp.float32), 'gamma0': jnp.ones((Cin,), jnp.float32), 'beta0': jnp.zeros((Cin,), jnp.float32), 'w0': jax.random.normal(ks[1], (Cout, Cin, 3, 3), jnp.float32) * 0.05, 'gamma1': jnp.ones((Cout,), jnp.float32), 'beta1': jnp.zeros((Cout,), jnp.float32), 'w1': jax.random.normal(ks[2], (Cout, Cout, 3, 3), jnp.float32) * 0.05}
    _L2_conv_all = _L2_conv_setup()
    _L2_conv_in = {k: v for k, v in _L2_conv_all.items() if k in ('gamma0', 'beta0', 'w0', 'gamma1', 'beta1', 'w1')}
    del _L2_conv_all

    def _L3_conv_setup():
        import jax, jax.numpy as jnp
        import numpy as np
        EPS = 1e-05
        key = jax.random.key(seed)
        k1, k2, k3 = jax.random.split(key, 3)
        B, C, H, W = (32, 64, 56, 56)
        Cq = C // 4
        x = jax.random.normal(k1, (B, C, H, W), jnp.float32)
        weight = jnp.eye(4, dtype=jnp.float32)[:, :, None] + 0.1 * jax.random.normal(k2, (4, 4, Cq), jnp.float32)
        bias = 0.1 * jax.random.normal(k3, (4, Cq), jnp.float32)
        return {'x': x, 'weight': weight, 'bias': bias}
    _L3_conv_all = _L3_conv_setup()
    _L3_conv_in = {k: v for k, v in _L3_conv_all.items() if k in ('weight', 'bias')}
    del _L3_conv_all
    return {'x': x, 'L0_conv_Wq': _L0_conv_in['Wq'], 'L0_conv_bq': _L0_conv_in['bq'], 'L0_conv_Wk': _L0_conv_in['Wk'], 'L0_conv_bk': _L0_conv_in['bk'], 'L0_conv_Wv': _L0_conv_in['Wv'], 'L0_conv_bv': _L0_conv_in['bv'], 'L0_conv_Wo': _L0_conv_in['Wo'], 'L0_conv_bo': _L0_conv_in['bo'], 'L0_conv_gamma': _L0_conv_in['gamma'], 'L1_conv_Wq': _L1_conv_in['Wq'], 'L1_conv_bq': _L1_conv_in['bq'], 'L1_conv_Wk': _L1_conv_in['Wk'], 'L1_conv_bk': _L1_conv_in['bk'], 'L1_conv_Wv': _L1_conv_in['Wv'], 'L1_conv_bv': _L1_conv_in['bv'], 'L2_conv_gamma0': _L2_conv_in['gamma0'], 'L2_conv_beta0': _L2_conv_in['beta0'], 'L2_conv_w0': _L2_conv_in['w0'], 'L2_conv_gamma1': _L2_conv_in['gamma1'], 'L2_conv_beta1': _L2_conv_in['beta1'], 'L2_conv_w1': _L2_conv_in['w1'], 'L3_conv_weight': _L3_conv_in['weight'], 'L3_conv_bias': _L3_conv_in['bias']}

def reference(x, L0_conv_Wq, L0_conv_bq, L0_conv_Wk, L0_conv_bk, L0_conv_Wv, L0_conv_bv, L0_conv_Wo, L0_conv_bo, L0_conv_gamma, L1_conv_Wq, L1_conv_bq, L1_conv_Wk, L1_conv_bk, L1_conv_Wv, L1_conv_bv, L2_conv_gamma0, L2_conv_beta0, L2_conv_w0, L2_conv_gamma1, L2_conv_beta1, L2_conv_w1, L3_conv_weight, L3_conv_bias):
    import jax
    import jax.numpy as jnp

    def _L0_conv_ref(x, Wq, bq, Wk, bk, Wv, bv, Wo, bo, gamma):
        import jax, jax.numpy as jnp
        import numpy as np
        B, C, W, H = x.shape
        N = W * H
        xf = x.reshape(B, C, N)
        q = jnp.einsum('oc,bcn->bno', Wq, xf) + bq
        k = jnp.einsum('oc,bcn->bon', Wk, xf) + bk[:, None]
        v = jnp.einsum('oc,bcn->bon', Wv, xf) + bv[:, None]
        energy = jnp.einsum('bno,bom->bnm', q, k)
        attn = jax.nn.softmax(energy, axis=-1)
        out = jnp.einsum('bcj,bij->bci', v, attn)
        out = jnp.einsum('oc,bcn->bon', Wo, out) + bo[:, None]
        out = out.reshape(B, C, W, H)
        return gamma * out + x

    def _L1_conv_ref(x, Wq, bq, Wk, bk, Wv, bv):
        import jax, jax.numpy as jnp
        import numpy as np
        TEMPERATURE = 1.0
        B, C, H, W = x.shape
        N = H * W
        xf = x.reshape(B, C, N)
        q = jnp.einsum('oc,bcn->bno', Wq, xf) + bq
        k = jnp.einsum('oc,bcn->bon', Wk, xf) + bk[:, None]
        attn = jax.nn.softmax(jnp.einsum('bno,bom->bnm', q, k), axis=-1)
        v = jnp.einsum('oc,bcn->bon', Wv, xf) + bv[:, None]
        out = jnp.einsum('bcn,bmn->bcm', v, attn).reshape(B, C, H, W)
        return x + out * TEMPERATURE

    def _L2_conv_ref(x, gamma0, beta0, w0, gamma1, beta1, w1):
        import jax, jax.numpy as jnp
        import numpy as np
        EPS = 1e-05

        def batch_norm(x, gamma, beta):
            mean = jnp.mean(x, axis=(0, 2, 3), keepdims=True)
            var = jnp.mean((x - mean) ** 2, axis=(0, 2, 3), keepdims=True)
            xhat = (x - mean) * jax.lax.rsqrt(var + EPS)
            return xhat * gamma[None, :, None, None] + beta[None, :, None, None]

        def quantize_w1bit(w):
            E = jax.lax.stop_gradient(jnp.mean(jnp.abs(w)))
            wq = E * jnp.sign(w)
            return w + jax.lax.stop_gradient(wq - w)

        def conv3x3(x, w):
            return jax.lax.conv_general_dilated(x, w, window_strides=(1, 1), padding=((1, 1), (1, 1)), dimension_numbers=('NCHW', 'OIHW', 'NCHW'))
        out = jax.nn.relu(batch_norm(x, gamma0, beta0))
        shortcut = x
        out = conv3x3(out, quantize_w1bit(w0))
        out = jax.nn.relu(batch_norm(out, gamma1, beta1))
        out = conv3x3(out, quantize_w1bit(w1))
        return out + shortcut

    def _L3_conv_ref(x, weight, bias):
        import jax, jax.numpy as jnp
        import numpy as np
        EPS = 1e-05
        B, C, H, W = x.shape
        Cq = C // 4
        N = B * H * W
        xq = jnp.transpose(x.reshape(B, 4, Cq, H, W), (1, 0, 2, 3, 4))
        mean = xq.mean(axis=(1, 3, 4))
        xc = xq - mean[:, None, :, None, None]
        perm = jnp.transpose(xc, (2, 0, 1, 3, 4)).reshape(Cq, 4, N)
        cov = jnp.einsum('cqn,cpn->cqp', perm, perm) / N
        A = cov + EPS * jnp.eye(4, dtype=x.dtype)
        L = jnp.linalg.cholesky(A)
        U = jnp.swapaxes(L, -1, -2)
        z = jax.scipy.linalg.solve_triangular(U, perm, lower=False)
        z = jnp.transpose(z.reshape(Cq, 4, B, H, W), (1, 2, 0, 3, 4))
        out = jnp.einsum('pqc,qbchw->pbchw', weight, z) + bias[:, None, :, None, None]
        return jnp.transpose(out, (1, 0, 2, 3, 4)).reshape(B, C, H, W)

    def _gn(v, G=32, eps=1e-05):
        B_, C_, H_, W_ = v.shape
        g = v.reshape(B_, G, C_ // G, H_, W_)
        m = jnp.mean(g, axis=(2, 3, 4), keepdims=True)
        s = jnp.var(g, axis=(2, 3, 4), keepdims=True)
        return ((g - m) / jnp.sqrt(s + eps)).reshape(v.shape)

    def _ln_c(v, eps=1e-06):
        m = jnp.mean(v, axis=1, keepdims=True)
        s = jnp.var(v, axis=1, keepdims=True)
        return (v - m) / jnp.sqrt(s + eps)

    def _ln_t(v, eps=1e-05):
        m = jnp.mean(v, axis=-1, keepdims=True)
        s = jnp.var(v, axis=-1, keepdims=True)
        return (v - m) / jnp.sqrt(s + eps)

    def _to_tokens(v):
        B_, C_, H_, W_ = v.shape
        return v.reshape(B_, C_, H_ * W_).transpose(0, 2, 1)

    def _from_tokens(t, like):
        B_, C_, H_, W_ = like.shape
        return t.transpose(0, 2, 1).reshape(B_, C_, H_, W_)
    x = _L0_conv_ref(x, L0_conv_Wq, L0_conv_bq, L0_conv_Wk, L0_conv_bk, L0_conv_Wv, L0_conv_bv, L0_conv_Wo, L0_conv_bo, L0_conv_gamma)
    x = _L1_conv_ref(x, L1_conv_Wq, L1_conv_bq, L1_conv_Wk, L1_conv_bk, L1_conv_Wv, L1_conv_bv)
    x = _L2_conv_ref(x, L2_conv_gamma0, L2_conv_beta0, L2_conv_w0, L2_conv_gamma1, L2_conv_beta1, L2_conv_w1)
    x = _L3_conv_ref(x, L3_conv_weight, L3_conv_bias)
    return x

_drawn_inputs = setup_inputs


def setup_inputs(seed=0):
    import zlib

    import numpy as np

    out = dict(_drawn_inputs(seed))
    spreads = {'L0_conv_bq': (0.0, 0.8),
     'L0_conv_bk': (0.0, 0.8),
     'L0_conv_bv': (0.0, 0.8),
     'L0_conv_bo': (0.0, 0.8),
     'L2_conv_gamma0': (1.0, 0.2),
     'L2_conv_beta0': (0.0, 0.1),
     'L2_conv_gamma1': (1.0, 0.2),
     'L2_conv_beta1': (0.0, 0.1)}
    factors = {'L1_conv_Wq': 8.0,
     'L1_conv_bq': 8.0,
     'L1_conv_Wk': 8.0,
     'L1_conv_bk': 8.0,
     'L1_conv_Wv': 4.996,
     'L1_conv_bv': 8.0}
    for name, (base, spread) in spreads.items():
        noise = np.random.default_rng([zlib.crc32(name.encode()), seed]).standard_normal(out[name].shape)
        drawn = base * np.exp(spread * noise) if base else spread * noise
        out[name] = jnp.asarray(drawn.astype(out[name].dtype))
    for name, factor in factors.items():
        out[name] = (out[name] * factor).astype(out[name].dtype)
    return out
```

```python
from contextlib import ExitStack

import concourse.bass as bass
import numpy as np
from concourse import mybir

F32 = mybir.dt.float32
F16 = mybir.dt.float16
BF16 = mybir.dt.bfloat16
U32 = mybir.dt.uint32
ALU = mybir.AluOpType
ACT = mybir.ActivationFunctionType
AX = mybir.AxisListType

P = 128
B, C, H, W = 8, 64, 16, 16
G = 2
PAIRS = B // G
N = H * W
CH = N // P
FREE = PAIRS * N
LAYERS = 2
ITERS = LAYERS * PAIRS
CQ = C // 8
CV = C // 2
AUG = 32
TAPS = 9
WP = W + 2
IMG = (H + 2) * WP
HALF = 512
IMGS = HALF // N
HALVES = FREE // HALF
Q = 4
CJ = C // Q
NTOT = B * N
BN_EPS = 1e-5
FP16_ROOM = 128.0

(P_BQ0, P_BK0, P_BQ1, P_BK1, P_GAMMA, P_BO, P_BV0, P_BV1, P_BNG0, P_BNB0, P_BNG1, P_BNB1,
 P_BIAS3) = range(13)
P_W3 = 13
P_COLS = P_W3 + Q * Q

K_ID = 0
K_AVG = K_ID + P
K_DIF = K_AVG + P
K_REP = K_DIF + P
K_ONES = K_REP + Q * P
K_MASKJ = K_ONES + P
K_MASKF = K_MASKJ + C
K_HOT = K_MASKF + P
K_EPSI = K_HOT + Q
K_MH = K_EPSI + Q * Q
K_COLS = K_MH + 1

A_Q0, A_K0, A_V0, A_O0, A_Q1, A_K1, A_V1 = (P * n for n in range(7))
A_COLS = 7 * P


def constants():
    part = np.arange(P)
    same_c = part[:, None] % C == part[None, :] % C
    same_g = part[:, None] // C == part[None, :] // C
    k = np.zeros((P, K_COLS), np.float32)
    k[:, K_ID:K_ID + P] = np.eye(P)
    k[:, K_AVG:K_AVG + P] = 0.5 * same_c
    k[:, K_DIF:K_DIF + P] = np.where(same_c, np.where(same_g, 0.5, -0.5), 0)
    for q in range(Q):
        k[:C, K_REP + q * P:K_REP + (q + 1) * P] = (
            (part[:C, None] // CJ == q) & (part[:C, None] % CJ == part[None, :] % CJ))
    k[:, K_ONES:K_ONES + P] = 1.0 / (P * C * TAPS)
    k[:, K_MASKJ:K_MASKJ + C] = part[:, None] % CJ == part[None, :C] % CJ
    k[:, K_MASKF:K_MASKF + P] = same_g & (part[:, None] % CJ == part[None, :] % CJ)
    k[:, K_HOT:K_HOT + Q] = (part[:, None] % C) // CJ == np.arange(Q)
    k[:, K_EPSI:K_EPSI + Q * Q] = BN_EPS * np.eye(Q).ravel()
    k[:, K_MH] = -0.5
    return k


def build(nc, x, attn_w, params, consts, conv_w, out):
    with ExitStack() as ctx:
        def sb(name, shape, dt=F32):
            return ctx.enter_context(nc.sbuf_tensor(name, shape, dt))

        def sem(name):
            return ctx.enter_context(nc.semaphore(name))

        xs = [sb(f"x{n}", [P, FREE]) for n in range(LAYERS + 1)]
        aw = sb("aw", [P, A_COLS])
        prm = sb("prm", [P, P_COLS])
        kst = sb("kst", [P, K_COLS])
        cw = [sb(f"cw{n}", [P, TAPS, C]) for n in range(2)]
        wv0 = sb("wv0", [P, P])
        const0 = sb("const0", [P, 1])
        qs = sb("qs", [P, 2, N])
        ks = sb("ks", [P, 2, N])
        vt = sb("vt", [P, 2, CH, 3 * C])
        negmax = sb("negmax", [P, 2, G, CH])
        probs = sb("probs", [P, 2, G, CH, N])
        recip = sb("recip", [P, N])
        mixed = sb("mixed", [P, N])
        stats = [sb(f"stats{n}", [P, 6 * k]) for n, k in ((0, PAIRS), (1, HALVES), (2, HALVES))]
        mv = [sb(f"mv{n}", [P, 2]) for n in range(3)]
        comb = [sb(f"comb{n}", [P, 3]) for n in range(3)]
        var = [sb(f"var{n}", [P, 1]) for n in range(2)]
        rstd = [sb(f"rstd{n}", [P, 1]) for n in range(2)]
        bn_s = [sb(f"bn_s{n}", [P, 1]) for n in range(2)]
        bn_b = [sb(f"bn_b{n}", [P, 1]) for n in range(2)]
        bn_t = [sb(f"bn_t{n}", [P, 8]) for n in range(2)]
        sign = [sb(f"sign{n}", [P, TAPS, C]) for n in range(2)]
        taps = [sb(f"taps{n}", [P, TAPS, P], BF16) for n in range(2)]
        wabs = [sb(f"wabs{n}", [P, 1]) for n in range(2)]
        emean = sb("emean", [P, 2])
        act32 = sb("act32", [P, FREE])
        act_hi = [sb(f"act_hi{n}", [P, PAIRS, H + 2, WP], F16) for n in range(2)]
        act_lo = [sb(f"act_lo{n}", [P, PAIRS, H + 2, WP], F16) for n in range(2)]
        y = sb("y", [P, FREE])
        yc = sb("yc", [P, FREE])
        yt = sb("yt", [P, FREE // P, P])
        gmask = sb("gmask", [C, Q, CJ])
        cov = sb("cov", [C, Q])
        tt = sb("tt", [P, Q, 2 * Q])
        upd = sb("upd", [P, Q, 2 * Q])
        piv = sb("piv", [P, Q])
        prod = sb("prod", [P, Q, Q])
        coef = sb("coef", [P, Q])
        final_w = sb("final_w", [P, G, Q, CJ])
        res = sb("res", [P, FREE])

        banks = [ctx.enter_context(nc.psum_tensor(f"bank{n}", [P, HALF], F32)) for n in range(8)]
        pb_qk, pb_v, pb_neg, pb_pv = banks[0], banks[1], banks[2], banks[3]
        pb_s, pb_t = banks[4:6], banks[6:8]
        pb_conv = [banks[0:2], banks[4:6]]
        pb_small = banks[3]
        pb_e = banks[2]
        pb_yt = [banks[0], banks[1]]
        pb_gram = banks[2]
        pb_out = banks[6:8]

        x_in = [sem(f"x_in{n}") for n in range(PAIRS)]
        aw_in, prm_in, kst_in = sem("aw_in"), sem("prm_in"), sem("kst_in")
        cw_in = [sem(f"cw_in{n}") for n in range(2)]
        ones_set = sem("ones_set")
        pads_set = sem("pads_set")
        wv0_mm, wv0_set = sem("wv0_mm"), sem("wv0_set")
        qk_mm, qk_out = sem("qk_mm"), sem("qk_out")
        v_mm, v_out = sem("v_mm"), sem("v_out")
        s_mm, max_out = sem("s_mm"), sem("max_out")
        neg_mm, neg_out = sem("neg_mm"), sem("neg_out")
        t_mm, exp_out = sem("t_mm"), sem("exp_out")
        pv_mm, pv_read, x_out = sem("pv_mm"), sem("pv_read"), sem("x_out")
        dve_step, w3_set = sem("dve_step"), sem("w3_set")
        sign_out, taps_out = sem("sign_out"), sem("taps_out")
        wabs_out, e_mm, e_out = sem("wabs_out"), sem("e_mm"), sem("e_out")
        bn_v = sem("bn_v")
        comb_mm = sem("comb_mm")
        var_out, rstd_out, bn_out = sem("var_out"), sem("rstd_out"), sem("bn_out")
        act_out, hi_out, lo_out = sem("act_out"), sem("hi_out"), sem("lo_out")
        conv_mm = sem("conv_mm")
        y_out, yc_out = sem("y_out"), sem("yc_out")
        yt_mm, yt_out = sem("yt_mm"), sem("yt_out")
        gram_mm, cov_out, rep_mm = sem("gram_mm"), sem("cov_out"), sem("rep_mm")
        piv_in, piv_out, chol = sem("piv_in"), sem("piv_out"), sem("chol")
        fw_out, fin_mm, res_out, stored = sem("fw_out"), sem("fin_mm"), sem("res_out"), sem("stored")

        block = ctx.enter_context(nc.Block())

        def x_of(i):
            lay, b = divmod(i, PAIRS)
            return xs[lay][:, b * N:(b + 1) * N]

        def wait_x(eng, i):
            if i < PAIRS:
                eng.wait_ge(x_in[i], 16)
            else:
                eng.wait_ge(x_out, i - PAIRS + 1)

        def padded(t, h):
            return t[:, h * IMGS:(h + 1) * IMGS, 1:H + 1, 1:W + 1]

        def imgs(ap):
            return ap.rearrange("p (b r w) -> p b r w", b=IMGS, r=H)

        @block.sync
        def _(sp):
            sp.dma_start(xs[0][:, 0:N], x[:, 0:N]).then_inc(x_in[0], 16)
            for b in range(1, PAIRS):
                sp.dma_start(xs[0][:, b * N:(b + 1) * N], x[:, b * N:(b + 1) * N]).then_inc(x_in[b], 16)
            for n in range(2):
                sp.dma_start(cw[n][:], conv_w[n].rearrange("p (t c) -> p t c", t=TAPS)).then_inc(cw_in[n], 16)
            for k in range(2 * HALVES):
                sp.wait_ge(res_out, k + 1)
                cols = slice(k * N, (k + 1) * N)
                sp.dma_start(out[:, cols], res[:, cols]).then_inc(stored, 16)
            sp.wait_ge(stored, 16 * 2 * HALVES)

        @block.gpsimd
        def _(pool):
            nc.gpsimd.memset(vt[:, :, :, C:2 * C], 1.0).then_inc(ones_set, 1)
            for n in range(2):
                nc.gpsimd.memset(taps[n][:], 0.0).then_inc(pads_set, 1)
                nc.gpsimd.memset(act_hi[n][:], 0.0).then_inc(pads_set, 1)
                nc.gpsimd.memset(act_lo[n][:], 0.0).then_inc(pads_set, 1)
            pool.wait_ge(kst_in, 16)
            mh = kst[:, K_MH:K_MH + 1]
            for n in range(2):
                pool.wait_ge(var_out, n + 1)
                nc.gpsimd.tensor_tensor(rstd[n][:], var[n][:], mh, ALU.pow).then_inc(rstd_out, 1)
            for j in range(Q):
                pool.wait_ge(piv_in, j + 1)
                nc.gpsimd.tensor_tensor(piv[:, j:j + 1], tt[:, j, j:j + 1], mh, ALU.pow).then_inc(piv_out, 1)

        @block.scalar
        def _(act):
            act.dma_start(aw[:, 0:4 * P], attn_w[:, 0:4 * P]).then_inc(aw_in, 16)
            act.dma_start(prm[:], params).then_inc(prm_in, 16)
            act.dma_start(kst[:], consts).then_inc(kst_in, 16)
            act.dma_start(aw[:, 4 * P:], attn_w[:, 4 * P:]).then_inc(aw_in, 16)
            act.wait_ge(prm_in, 16)

            act.wait_ge(wv0_mm, 1)
            nc.scalar.activation(wv0[:], pb_e[:, 0:P], ACT.Identity,
                                 scale=prm[:, P_GAMMA:P_GAMMA + 1]).then_inc(wv0_set, 1)

            def project_out(i):
                act.wait_ge(qk_mm, i + 1)
                if i >= 2:
                    act.wait_ge(t_mm, 2 * (i - 1))
                bq, bk = (P_BQ0, P_BK0) if i < PAIRS else (P_BQ1, P_BK1)
                nc.scalar.activation(qs[:, i % 2, :], pb_qk[:, 0:N], ACT.Identity,
                                     bias=prm[:, bq:bq + 1]).then_inc(qk_out, 1)
                nc.scalar.activation(ks[:, i % 2, :], pb_qk[:, N:2 * N], ACT.Identity,
                                     bias=prm[:, bk:bk + 1]).then_inc(qk_out, 1)

            def exps(i):
                if i >= 2:
                    act.wait_ge(pv_mm, i - 1)
                for g in range(G):
                    act.wait_ge(t_mm, 2 * i + g + 1)
                    nc.scalar.activation(probs[:, i % 2, g], pb_t[g][:].rearrange("p (t n) -> p t n", t=CH),
                                         ACT.Exp).then_inc(exp_out, 1)

            def values_out(i):
                act.wait_ge(v_mm, i + 1)
                if i >= 2:
                    act.wait_ge(pv_mm, i - 1)
                dst = vt[:, i % 2].rearrange("p t (g c) -> p t g c", g=3)[:, :, 0:3:2, :]
                nc.scalar.activation(dst, pb_v[:, 0:CH * P].rearrange("p (t g c) -> p t g c", t=CH, g=G),
                                     ACT.Identity).then_inc(v_out, 1)

            def neg_out_rows(i):
                act.wait_ge(neg_mm, i + 1)
                for g in range(G):
                    row = C * g + AUG
                    nc.scalar.activation(qs[row:row + 1, i % 2, :], pb_neg[0:1, g * N:(g + 1) * N],
                                         ACT.Identity).then_inc(neg_out, 1)

            for i in range(-2, ITERS):
                if i + 2 < ITERS:
                    project_out(i + 2)
                if i >= 0:
                    exps(i)
                if 0 <= i + 1 < ITERS:
                    values_out(i + 1)
                    neg_out_rows(i + 1)
                if i in (0, 1):
                    act.wait_ge(cw_in[i], 16)
                    nc.scalar.activation(sign[i][:], cw[i][:], ACT.Sign).then_inc(sign_out, 1)

            for n in range(2):
                act.wait_ge(bn_out, n + 1)
                for h in range(HALVES):
                    cols = slice(h * HALF, (h + 1) * HALF)
                    src = xs[LAYERS][:, cols] if n == 0 else pb_conv[0][h][:]
                    if n == 1:
                        act.wait_ge(lo_out, h + 1)
                    nc.scalar.activation(act32[:, cols], src, ACT.Relu, scale=bn_s[n][:],
                                         bias=bn_b[n][:]).then_inc(act_out, 1)
            act.wait_ge(yt_mm, 1)
            nc.scalar.activation(yt[:, 0:4, :], pb_yt[0][:].rearrange("p (k c) -> p k c", k=4),
                                 ACT.Identity).then_inc(yt_out, 1)
            for h in range(HALVES):
                act.wait_ge(fin_mm, h + 1)
                for s in range(2):
                    nc.scalar.activation(res[:, h * HALF + s * N:h * HALF + (s + 1) * N],
                                         pb_out[h][:, s * N:(s + 1) * N], ACT.Identity,
                                         bias=prm[:, P_BIAS3:P_BIAS3 + 1]).then_inc(res_out, 1)

        @block.tensor
        def _(pe):
            mm = nc.tensor.matmul
            ident = kst[:, K_ID:K_ID + P]
            pe.wait_ge(aw_in, 32)
            mm(pb_e[:, 0:P], aw[0:C, A_V0:A_V0 + P], aw[0:C, A_O0:A_O0 + P], start=True, stop=True)
            pe.wait_ge(prm_in, 16)
            mm(pb_e[:, P:P + 1], aw[0:C, A_O0:A_O0 + P], prm[0:C, P_BV0:P_BV0 + 1],
               start=True, stop=True).then_inc(wv0_mm, 1)

            def project(i):
                wait_x(pe, i)
                if i >= 1:
                    pe.wait_ge(qk_out, 2 * i)
                q0, k0 = (A_Q0, A_K0) if i < PAIRS else (A_Q1, A_K1)
                mm(pb_qk[:, 0:N], aw[:, q0:q0 + P], x_of(i), start=True, stop=True)
                mm(pb_qk[:, N:2 * N], aw[:, k0:k0 + P], x_of(i), start=True, stop=True).then_inc(qk_mm, 1)

            def values(i):
                wait_x(pe, i)
                if i >= 1:
                    pe.wait_ge(v_out, i)
                if i == 0:
                    pe.wait_ge(wv0_set, 1)
                wv = wv0[:] if i < PAIRS else aw[:, A_V1:A_V1 + P]
                for t in range(CH):
                    last = mm(pb_v[:, t * P:(t + 1) * P], x_of(i)[:, t * P:(t + 1) * P], wv,
                              start=True, stop=True)
                last.then_inc(v_mm, 1)

            def scores(i):
                pe.wait_ge(qk_out, 2 * i + 2)
                for g in range(G):
                    if i >= 1:
                        pe.wait_ge(max_out, 2 * i - 1 + g)
                    rows = slice(C * g, C * (g + 1))
                    for t in range(CH):
                        last = mm(pb_s[g][:, t * N:(t + 1) * N], qs[rows, i % 2, t * P:(t + 1) * P],
                                  ks[rows, i % 2, :], start=True, stop=True)
                    last.then_inc(s_mm, 1)

            def scores_t(i):
                pe.wait_ge(neg_out, 2 * i + 2)
                for g in range(G):
                    if i >= 1:
                        pe.wait_ge(exp_out, 2 * i - 1 + g)
                    rows = slice(C * g, C * (g + 1))
                    for t in range(CH):
                        last = mm(pb_t[g][:, t * N:(t + 1) * N], ks[rows, i % 2, t * P:(t + 1) * P],
                                  qs[rows, i % 2, :], start=True, stop=True)
                    last.then_inc(t_mm, 1)

            def maxima_to_rows(i):
                pe.wait_ge(max_out, 2 * i + 2)
                if i >= 1:
                    pe.wait_ge(neg_out, 2 * i)
                if i == 0:
                    pe.wait_ge(kst_in, 16)
                for g in range(G):
                    for t in range(CH):
                        col = g * N + t * P
                        last = nc.tensor.transpose(pb_neg[0:1, col:col + P], negmax[:, i % 2, g, t:t + 1], ident)
                last.then_inc(neg_mm, 1)

            def mix(i):
                pe.wait_ge(v_out, i + 1)
                if i == 0:
                    pe.wait_ge(ones_set, 1)
                if i >= 1:
                    pe.wait_ge(pv_read, i)
                for g in range(G):
                    pe.wait_ge(exp_out, 2 * i + g + 1)
                    for t in range(CH):
                        last = mm(pb_pv[:, g * N:(g + 1) * N], vt[:, i % 2, t, g * C:g * C + P],
                                  probs[:, i % 2, g, t, :], start=(t == 0), stop=(t == CH - 1))
                last.then_inc(pv_mm, 1)

            for i in range(-2, ITERS):
                if i + 2 < ITERS:
                    project(i + 2)
                if 0 <= i + 1 < ITERS:
                    scores(i + 1)
                if i >= 0:
                    scores_t(i)
                if 0 <= i + 1 < ITERS:
                    values(i + 1)
                    maxima_to_rows(i + 1)
                if i >= 0:
                    mix(i)

            def combine(n):
                mm(pb_small[:, 0:2], kst[:, K_AVG:K_AVG + P], mv[n][:], start=True, stop=True)
                mm(pb_small[:, 2:3], kst[:, K_DIF:K_DIF + P], mv[n][:, 0:1], start=True,
                   stop=True).then_inc(comb_mm, 1)

            pe.wait_ge(wabs_out, 2)
            for n in range(2):
                last = mm(pb_e[:, n:n + 1], kst[:, K_ONES:K_ONES + P], wabs[n][:], start=True, stop=True)
            last.then_inc(e_mm, 1)
            pe.wait_ge(bn_v, 1)
            pe.wait_ge(pv_read, ITERS)
            combine(0)
            for n in range(2):
                pe.wait_ge(taps_out, 2 * n + 2)
                for h in range(HALVES):
                    for part, (src, ready) in enumerate(((act_hi[n], hi_out), (act_lo[n], lo_out))):
                        pe.wait_ge(ready, n * HALVES + h + 1)
                        for k in range(TAPS):
                            dy, dx = divmod(k, 3)
                            last = mm(imgs(pb_conv[n][h][:]), taps[n][:, k, :],
                                      src[:, h * IMGS:(h + 1) * IMGS, dy:dy + H, dx:dx + W],
                                      start=(part == 0 and k == 0), stop=(part == 1 and k == TAPS - 1))
                    last.then_inc(conv_mm, 1)
                if n == 0:
                    pe.wait_ge(bn_v, 2)
                    combine(1)
            pe.wait_ge(bn_v, 3)
            mm(pb_small[:, 0:2], kst[:, K_AVG:K_AVG + P], mv[2][:], start=True, stop=True).then_inc(comb_mm, 1)

            for h in range(2):
                pe.wait_ge(yc_out, h + 1)
                for k in range(4):
                    col = (4 * h + k) * P
                    last = nc.tensor.transpose(pb_yt[h][:, k * P:(k + 1) * P], yc[:, col:col + P], ident)
                last.then_inc(yt_mm, 1)
            pe.wait_ge(yt_out, 2)
            for k in range(FREE // P):
                for g in range(G):
                    z = yt[:, k, g * C:(g + 1) * C]
                    last = mm(pb_gram[0:C, 0:C], z, z, start=(k == 0 and g == 0),
                              stop=(k == FREE // P - 1 and g == G - 1))
            last.then_inc(gram_mm, 1)
            pe.wait_ge(cov_out, 1)
            for q in range(Q):
                last = mm(pb_small[:, 8 + q * Q:8 + (q + 1) * Q], kst[0:C, K_REP + q * P:K_REP + (q + 1) * P],
                          cov[:], start=True, stop=True)
            last.then_inc(rep_mm, 1)
            pe.wait_ge(fw_out, 1)
            for h in range(HALVES):
                mm(pb_out[h][:], final_w[:].rearrange("p g q j -> p (g q j)"),
                   yc[:, h * HALF:(h + 1) * HALF], start=True, stop=True).then_inc(fin_mm, 1)

        @block.vector
        def _(dve):
            ve = nc.vector
            steps = [0]

            def step(ins):
                ins.then_inc(dve_step, 1)
                steps[0] += 1
                dve.wait_ge(dve_step, steps[0])

            dve.wait_ge(prm_in, 16)
            for n, (g_, b_) in enumerate(((P_BNG0, P_BNB0), (P_BNG1, P_BNB1))):
                t = bn_t[n]
                step(ve.tensor_reduce(t[:, 0:1], prm[:, g_:b_ + 1], AX.X, ALU.max, apply_absolute_value=True))
                step(ve.tensor_scalar(t[:, 1:2], t[:, 0:1], 1e-30, 1.0 / FP16_ROOM, ALU.max, ALU.mult))
                step(ve.tensor_scalar(t[:, 2:3].bitcast(U32), t[:, 1:2].bitcast(U32), 0x7F800000, None,
                                      ALU.bitwise_and))
                step(ve.reciprocal(t[:, 3:4], t[:, 2:3]))
                step(ve.tensor_scalar(t[:, 4:6], prm[:, g_:b_ + 1], t[:, 3:4], None, ALU.mult))
            ve.tensor_copy(tt[:, :, Q:2 * Q],
                           prm[:, P_W3:P_W3 + Q * Q].rearrange("p (i r) -> p i r", i=Q)).then_inc(w3_set, 1)
            dve.wait_ge(wv0_set, 1)
            step(ve.tensor_scalar(const0[:], pb_e[:, P:P + 1], prm[:, P_BO:P_BO + 1],
                                  prm[:, P_GAMMA:P_GAMMA + 1], ALU.add, ALU.mult))

            def maxima(i):
                if i >= 2:
                    dve.wait_ge(neg_mm, i - 1)
                for g in range(G):
                    dve.wait_ge(s_mm, 2 * i + g + 1)
                    ve.tensor_reduce(negmax[:, i % 2, g, :], pb_s[g][:].rearrange("p (t n) -> p t n", t=CH),
                                     AX.X, ALU.max, negate=True).then_inc(max_out, 1)

            def normalise(i):
                lay, b = divmod(i, PAIRS)
                dve.wait_ge(pv_mm, i + 1)
                lo, hi = slice(0, C), slice(C, P)
                ve.reciprocal(recip[lo, :], pb_pv[hi, 0:N])
                step(ve.reciprocal(recip[hi, :], pb_pv[lo, N:2 * N]))
                ve.tensor_tensor(mixed[lo, :], pb_pv[lo, 0:N], recip[lo, :], ALU.mult)
                ve.tensor_tensor(mixed[hi, :], pb_pv[hi, N:2 * N], recip[hi, :], ALU.mult).then_inc(pv_read, 1)
                dve.wait_ge(pv_read, i + 1)
                const = const0[:] if lay == 0 else prm[:, P_BV1:P_BV1 + 1]
                cols = slice(b * N, (b + 1) * N)
                ve.scalar_tensor_tensor(xs[lay + 1][:, cols], mixed[:], const, xs[lay][:, cols],
                                        ALU.add, ALU.add).then_inc(x_out, 1)
                if lay == LAYERS - 1:
                    dve.wait_ge(x_out, i + 1)
                    step(ve.bn_stats(stats[0][:, 6 * b:6 * b + 6], xs[LAYERS][:, cols]))

            def conv_weights(n):
                dve.wait_ge(cw_in[n], 16)
                ve.tensor_reduce(wabs[n][:], cw[n][:], AX.XY, ALU.add,
                                 apply_absolute_value=True).then_inc(wabs_out, 1)
                dve.wait_ge(sign_out, n + 1)
                dve.wait_ge(pads_set, 3 * n + 1)
                for g in range(G):
                    rows = slice(g * C, (g + 1) * C)
                    ve.tensor_scalar(taps[n][rows, :, g * C:(g + 1) * C], sign[n][rows], bn_t[n][rows, 2:3],
                                     None, ALU.mult).then_inc(taps_out, 1)

            for i in range(-2, ITERS):
                if 0 <= i + 1 < ITERS:
                    maxima(i + 1)
                if i >= 0:
                    normalise(i)
                if i in (0, 1):
                    conv_weights(i)

            dve.wait_ge(e_mm, 1)
            step(ve.tensor_copy(emean[:], pb_e[:, 0:2]))
            step(ve.tensor_scalar(bn_t[1][:, 4:5], bn_t[1][:, 4:5], emean[:, 0:1], None, ALU.mult))
            step(ve.tensor_tensor(bn_t[1][:, 6:7], emean[:, 0:1], emean[:, 0:1], ALU.mult))

            for n in range(2):
                if n == 1:
                    for h in range(HALVES):
                        dve.wait_ge(conv_mm, h + 1)
                        step(ve.bn_stats(stats[1][:, 6 * h:6 * h + 6], pb_conv[0][h][:]))
                ve.bn_aggr(mv[n][:], stats[n][:]).then_inc(bn_v, 1)
                dve.wait_ge(comb_mm, n + 1)
                t, c = bn_t[n], comb[n]
                step(ve.tensor_copy(c[:], pb_small[:, 0:3]))
                step(ve.scalar_tensor_tensor(var[n][:], c[:, 2:3], c[:, 2:3], c[:, 1:2], ALU.mult, ALU.add))
                factor = 1.0 if n == 0 else t[:, 6:7]
                ve.tensor_scalar(var[n][:], var[n][:], factor, BN_EPS, ALU.mult, ALU.add).then_inc(var_out, 1)
                dve.wait_ge(rstd_out, n + 1)
                step(ve.tensor_tensor(bn_s[n][:], t[:, 4:5], rstd[n][:], ALU.mult))
                ve.scalar_tensor_tensor(bn_b[n][:], c[:, 0:1], bn_s[n][:], t[:, 5:6], ALU.mult, ALU.subtract,
                                        reverse1=True).then_inc(bn_out, 1)
                dve.wait_ge(pads_set, 6)
                for h in range(HALVES):
                    cols = slice(h * HALF, (h + 1) * HALF)
                    dve.wait_ge(act_out, n * HALVES + h + 1)
                    ve.tensor_copy(padded(act_hi[n], h), imgs(act32[:, cols])).then_inc(hi_out, 1)
                    dve.wait_ge(hi_out, n * HALVES + h + 1)
                    ve.tensor_tensor(padded(act_lo[n], h), imgs(act32[:, cols]), padded(act_hi[n], h),
                                     ALU.subtract).then_inc(lo_out, 1)

            for h in range(HALVES):
                cols = slice(h * HALF, (h + 1) * HALF)
                dve.wait_ge(conv_mm, HALVES + h + 1)
                step(ve.scalar_tensor_tensor(y[:, cols], pb_conv[1][h][:], emean[:, 1:2], xs[LAYERS][:, cols],
                                             ALU.mult, ALU.add))
                step(ve.bn_stats(stats[2][:, 6 * h:6 * h + 6], y[:, cols]))
            ve.bn_aggr(mv[2][:], stats[2][:]).then_inc(bn_v, 1)
            dve.wait_ge(comb_mm, 3)
            step(ve.tensor_copy(comb[2][:, 0:2], pb_small[:, 0:2]))
            for h in range(HALVES):
                cols = slice(h * HALF, (h + 1) * HALF)
                ve.tensor_scalar(yc[:, cols], y[:, cols], comb[2][:, 0:1], None, ALU.subtract).then_inc(yc_out, 1)
            dve.wait_ge(yt_mm, 2)
            ve.tensor_copy(yt[:, 4:8, :], pb_yt[1][:].rearrange("p (k c) -> p k c", k=4)).then_inc(yt_out, 1)
            dve.wait_ge(gram_mm, 1)
            step(ve.tensor_tensor(gmask[:].rearrange("p q j -> p (q j)"), pb_gram[0:C, 0:C],
                                  kst[0:C, K_MASKJ:K_MASKJ + C], ALU.mult))
            ve.tensor_reduce(cov[:], gmask[:], AX.X, ALU.add).then_inc(cov_out, 1)
            dve.wait_ge(rep_mm, 1)
            dve.wait_ge(w3_set, 1)
            step(ve.scalar_tensor_tensor(tt[:, :, 0:Q], pb_small[:, 8:8 + Q * Q].rearrange("p (i r) -> p i r", i=Q),
                                         1.0 / NTOT,
                                         kst[:, K_EPSI:K_EPSI + Q * Q].rearrange("p (i r) -> p i r", i=Q),
                                         ALU.mult, ALU.add))
            for j in range(Q):
                ve.engine_nop().then_inc(piv_in, 1)
                dve.wait_ge(piv_out, j + 1)
                step(ve.tensor_scalar(tt[:, j, j:], tt[:, j, j:], piv[:, j:j + 1], None, ALU.mult))
                if j < Q - 1:
                    left, rows = Q - 1 - j, 2 * Q - 1 - j
                    col = tt[:, j:j + 1, j + 1:].to_broadcast([P, left, rows])
                    lij = tt[:, j, j + 1:Q].unsqueeze(2).to_broadcast([P, left, rows])
                    step(ve.tensor_tensor(upd[:, j + 1:, j + 1:], col, lij, ALU.mult))
                    step(ve.tensor_tensor(tt[:, j + 1:, j + 1:], tt[:, j + 1:, j + 1:], upd[:, j + 1:, j + 1:],
                                          ALU.subtract))
            hot = kst[:, K_HOT:K_HOT + Q].unsqueeze(1).to_broadcast([P, Q, Q])
            step(ve.tensor_tensor(prod[:], tt[:, :, Q:2 * Q].rearrange("p i r -> p r i"), hot, ALU.mult))
            step(ve.tensor_reduce(coef[:], prod[:], AX.X, ALU.add))
            spread = coef[:].unsqueeze(1).unsqueeze(3).to_broadcast([P, G, Q, CJ])
            ve.tensor_tensor(final_w[:], kst[:, K_MASKF:K_MASKF + P].rearrange("p (g q j) -> p g q j", g=G, q=Q),
                             spread, ALU.mult).then_inc(fw_out, 1)


def kernel(**inputs):
    import concourse.bacc as bacc
    from concourse.bass_utils import run_bass_kernel_spmd

    a = {name: np.asarray(v) for name, v in inputs.items()}

    def halves(m):
        return np.concatenate([m, m], axis=0)

    def diagonal(m, rows=C):
        out = np.zeros((P, P), m.dtype)
        out[0:m.shape[0], 0:m.shape[1]] = m
        out[rows:rows + m.shape[0], C:C + m.shape[1]] = m
        return out

    x = a["x"].reshape(G, PAIRS, C, N).transpose(0, 2, 1, 3).reshape(P, FREE)
    attn_w = np.concatenate([
        diagonal(a["L0_conv_Wq"].T), diagonal(a["L0_conv_Wk"].T),
        diagonal(a["L0_conv_Wv"], CV), diagonal(a["L0_conv_Wo"].T, CV),
        diagonal(a["L1_conv_Wq"].T), diagonal(a["L1_conv_Wk"].T), diagonal(a["L1_conv_Wv"].T)], axis=1)
    params = np.zeros((P, P_COLS), np.float32)
    for g in range(G):
        row = g * C
        for lay, (pq, pk) in enumerate(((P_BQ0, P_BK0), (P_BQ1, P_BK1))):
            params[row:row + CQ, pq] = a[f"L{lay}_conv_bq"]
            params[row:row + CQ, pk] = a[f"L{lay}_conv_bk"]
            params[row + AUG, pk] = 1.0
        params[g * CV:(g + 1) * CV, P_BV0] = a["L0_conv_bv"]
    params[:, P_GAMMA] = a["L0_conv_gamma"][0]
    for col, name in ((P_BO, "L0_conv_bo"), (P_BV1, "L1_conv_bv"), (P_BNG0, "L2_conv_gamma0"),
                      (P_BNB0, "L2_conv_beta0"), (P_BNG1, "L2_conv_gamma1"), (P_BNB1, "L2_conv_beta1")):
        params[:, col] = halves(a[name])
    params[:, P_BIAS3] = halves(a["L3_conv_bias"].reshape(C))
    w3 = a["L3_conv_weight"].transpose(2, 1, 0).reshape(CJ, Q * Q)
    params[:, P_W3:P_W3 + Q * Q] = np.concatenate([w3] * (G * Q), axis=0)
    conv_w = [halves(a[f"L2_conv_w{n}"].reshape(C, C, TAPS).transpose(1, 2, 0).reshape(C, TAPS * C))
              for n in range(2)]

    nc = bacc.Bacc("TRN2", target_bir_lowering=False, num_devices=1)
    arrays = {"x_in": x, "attn_w": attn_w, "params": params, "consts": constants(),
              "conv_w0": conv_w[0], "conv_w1": conv_w[1]}
    arrays = {name: np.ascontiguousarray(v) for name, v in arrays.items()}
    t = {name: nc.dram_tensor(name, v.shape, mybir.dt.from_np(v.dtype), kind="ExternalInput").ap()
         for name, v in arrays.items()}
    out = nc.dram_tensor("out", (P, FREE), F32, kind="ExternalOutput").ap()
    build(nc, t["x_in"], t["attn_w"], t["params"], t["consts"], [t["conv_w0"], t["conv_w1"]], out)
    r = run_bass_kernel_spmd(nc, [arrays], core_ids=[0])
    got = r.results[0]["out"]
    return got.reshape(G, C, PAIRS, N).transpose(0, 2, 1, 3).reshape(B, C, H, W)
```

```python
from contextlib import ExitStack

import concourse.bass as bass
import numpy as np
from concourse import mybir

F32 = mybir.dt.float32
F16 = mybir.dt.float16
BF16 = mybir.dt.bfloat16
U32 = mybir.dt.uint32
ALU = mybir.AluOpType
ACT = mybir.ActivationFunctionType
AX = mybir.AxisListType

P = 128
B, C, H, W = 8, 64, 16, 16
G = 2
PAIRS = B // G
N = H * W
CH = N // P
FREE = PAIRS * N
LAYERS = 2
ITERS = LAYERS * PAIRS
CQ = C // 8
CV = C // 2
PARTS = ((0, 0), (0, 1), (1, 0), (1, 1), (0, 2), (2, 0), (1, 2), (2, 1))
SPLIT = 3
DEPTH = 4
TAPS = 9
WP = W + 2
IMG = (H + 2) * WP
HALF = 512
Q = 4
CJ = C // Q
NTOT = B * N
BN_EPS = 1e-5
WARM = (4, 15, 2, 14, 3, 15)
WARM_START = (8, 4, 4, 4)
WARM_ATTENTION = (3, 2, 1)
E_SQUARE_MIN = 1e-37
FP16_ROOM = 128.0

(P_BQ0, P_BK0, P_BQ1, P_BK1, P_GAMMA, P_BO, P_BV0, P_BV1, P_BNG0, P_BNB0, P_BNG1, P_BNB1,
 P_BIAS3, P_MQ1, P_MQ2, P_MK1, P_MK2) = range(17)
P_W3 = 17
P_COLS = P_W3 + Q * Q

K_ID = 0
K_MH = K_ID + P
K_FIRST = K_MH + 1
K_AVG = K_FIRST
K_DIF = K_AVG + P
K_REP = K_DIF + P
K_ONES = K_REP + P
K_MASKJ = K_ONES + P
K_MASKF = K_MASKJ + C
K_HOT = K_MASKF + P
K_EPSN = K_HOT + Q
K_COLS = K_EPSN + C + 1
SHIFTS = SPLIT * G * CH

A_Q0, A_K0, A_V0, A_O0, A_Q1, A_K1, A_V1 = (P * n for n in range(7))
A_COLS = 7 * P


def constants():
    part = np.arange(P)
    same_c = part[:, None] % C == part[None, :] % C
    same_g = part[:, None] // C == part[None, :] // C
    k = np.zeros((P, K_COLS), np.float32)
    k[:, K_ID:K_ID + P] = np.eye(P)
    k[:, K_AVG:K_AVG + P] = 0.5 * same_c
    k[:, K_DIF:K_DIF + P] = np.where(same_c, np.where(same_g, 0.5, -0.5), 0)
    k[:C, K_REP:K_REP + P] = (part[:C, None] % CJ == part[None, :] % CJ) / NTOT
    k[:, K_ONES:K_ONES + P] = 1.0 / (P * C * TAPS)
    k[:, K_MASKJ:K_MASKJ + C] = part[:, None] % CJ == part[None, :C] % CJ
    k[:, K_MASKF:K_MASKF + P] = same_g & (part[:, None] % CJ == part[None, :] % CJ)
    k[:, K_HOT:K_HOT + Q] = (part[:, None] % C) // CJ == np.arange(Q)
    k[:C, K_EPSN:K_EPSN + C] = BN_EPS * NTOT * np.eye(C)
    k[:, K_MH] = -0.5
    return k


def selectors():
    rows = np.arange(SHIFTS)[:, None, None] % (G * CH)
    return np.broadcast_to(rows == np.arange(G * CH)[None, :, None], (SHIFTS, G * CH, P)).astype(np.float32)


def build(nc, x, attn_w, params, consts, select, conv_w, out):
    with ExitStack() as ctx:
        def sb(name, shape, dt=F32):
            return ctx.enter_context(nc.sbuf_tensor(name, shape, dt))

        def sem(name):
            return ctx.enter_context(nc.semaphore(name))

        xs = [sb(f"x{n}", [P, FREE]) for n in range(LAYERS + 1)]
        aw = sb("aw", [P, A_COLS])
        prm = sb("prm", [P, P_COLS])
        kst = sb("kst", [P, K_COLS])
        sel = sb("sel", [SHIFTS, G * CH, P])
        cw = [sb(f"cw{n}", [P, TAPS, C]) for n in range(2)]
        wv0 = sb("wv0", [P, P])
        const0 = sb("const0", [P, 1])
        proj = sb("proj", [P, 2, 2, N])
        cut1 = sb("cut1", [P, 2, N], BF16)
        rest = sb("rest", [P, 2, N])
        cut2 = sb("cut2", [P, 2, N], BF16)
        qk = sb("qk", [P, DEPTH, 2, N], BF16)
        vt = sb("vt", [P, 2, CH, P])
        negmax = sb("negmax", [P, 2, G * CH])
        junk = sb("junk", [P, G * CH, N], BF16)
        total = sb("total", [P, 2, G * CH])
        lntot = sb("lntot", [P, 2, G * CH])
        shift = sb("shift", [P, G * CH])
        shift_r = sb("shift_r", [P, G * CH])
        shift_p = sb("shift_p", [P, 2, SPLIT, G * CH], BF16)
        shift_t = sb("shift_t", [SHIFTS, 2, P], BF16)
        sel16 = sb("sel16", [SHIFTS, G * CH, P], BF16)
        probs = sb("probs", [P, 2, G, CH, N])
        ident16 = sb("ident16", [P, P], BF16)
        stats = [sb(f"stats{n}", [P, 6 * k]) for n, k in ((0, PAIRS), (1, PAIRS), (2, 1))]
        mv = [sb(f"mv{n}", [P, 2]) for n in range(3)]
        npre = sb("npre", [P, 1])
        var = [sb(f"var{n}", [P, 1]) for n in range(2)]
        rstd = [sb(f"rstd{n}", [P, 1]) for n in range(2)]
        bn_s = [sb(f"bn_s{n}", [P, 1]) for n in range(2)]
        bn_b = [sb(f"bn_b{n}", [P, 1]) for n in range(2)]
        bn_t = [sb(f"bn_t{n}", [P, 8]) for n in range(2)]
        sign = [sb(f"sign{n}", [P, TAPS, C]) for n in range(2)]
        taps = [sb(f"taps{n}", [P, TAPS, C], BF16) for n in range(2)]
        wabs = [sb(f"wabs{n}", [P, 1]) for n in range(2)]
        esq, einv, eps1 = (sb(name, [P, 1]) for name in ("esq", "einv", "eps1"))
        emean = sb("emean", [P, 2])
        z0 = sb("z0", [P, N])
        act32 = sb("act32", [P, FREE])
        conv_in = [[sb(f"conv_in{n}{g}", [P, PAIRS, H + 2, WP], F16) for g in range(G)] for n in range(2)]
        xc = sb("xc", [P, FREE])
        yc = sb("yc", [P, FREE])
        warm = sb("warm", [P, HALF], BF16)
        yt = sb("yt", [P, FREE // P, G, C + 1])
        gmask = sb("gmask", [C, Q, CJ])
        cov = sb("cov", [C, Q + 1])
        cov_q = sb("cov_q", [C, Q, Q + 1])
        dmean = sb("dmean", [P, 1])
        means = sb("means", [P, Q])
        dd = sb("dd", [P, Q, Q])
        own = sb("own", [P, Q])
        bias3 = sb("bias3", [P, 1])
        tt = sb("tt", [P, Q, 2 * Q])
        upd = sb("upd", [P, Q, 2 * Q])
        inv = sb("inv", [P, Q - 1])
        dpiv = sb("dpiv", [P, 1])
        piv = sb("piv", [P, 1])
        prod = sb("prod", [P, Q, Q])
        coef = sb("coef", [P, Q])
        placed = sb("placed", [P, G, Q, CJ])
        final_w = sb("final_w", [P, G, Q, CJ])
        res = sb("res", [P, FREE])

        banks = [ctx.enter_context(nc.psum_tensor(f"bank{n}", [P, HALF], F32)) for n in range(8)]
        pb_qk, pb_v, pb_pv = banks[0], banks[1], banks[3]
        pb_shift = pb_v[:].bitcast(BF16)[:, 4 * P:5 * P]
        pb_s, pb_t = [banks[n] for n in (2, 4, 5)], banks[6:8]
        pb_conv = [[banks[n] for n in ns] for ns in ((0, 1, 4, 5), (6, 7, 2, 0))]
        pb_small = banks[3]
        pb_e = banks[2]
        pb_yt = banks[4:6]
        pb_gram = banks[1]
        pb_out = pb_conv[1]
        pb_warm = banks[6]
        pb_mean = banks[7]
        R_COL = 8
        pb_bias = banks[4]

        x_in = [sem(f"x_in{n}") for n in range(PAIRS)]
        qk0_in, vo0_in, aw1_in = sem("qk0_in"), sem("vo0_in"), sem("aw1_in")
        prm_in, id_in, sel_in, kst_in = sem("prm_in"), sem("id_in"), sem("sel_in"), sem("kst_in")
        cw_in = [sem(f"cw_in{n}") for n in range(2)]
        pads_set = sem("pads_set")
        wv0_mm, wv0_set, const0_set = sem("wv0_mm"), sem("wv0_set"), sem("const0_set")
        qk_mm, qk_out = sem("qk_mm"), sem("qk_out")
        v_mm, v_out = sem("v_mm"), sem("v_out")
        s_mm, max_out = sem("s_mm"), sem("max_out")
        parts_out = sem("parts_out")
        total_out, ln_out, shift_out = sem("total_out"), sem("ln_out"), sem("shift_out")
        rows_mm, rows_out = sem("rows_mm"), sem("rows_out")
        id16_set, sel_set = sem("id16_set"), sem("sel_set")
        pow2_out = sem("pow2_out")
        cut_out, rest_out = sem("cut_out"), sem("rest_out")
        t_mm, exp_out = sem("t_mm"), sem("exp_out")
        pv_mm, x_out = sem("pv_mm"), sem("x_out")
        dve_step, w3_set = sem("dve_step"), sem("w3_set")
        sign_out, taps_out = sem("sign_out"), sem("taps_out")
        wabs_out, e_mm = sem("wabs_out"), sem("e_mm")
        bn_v = sem("bn_v")
        comb_mm = sem("comb_mm")
        var_out, rstd_out, bn_out = sem("var_out"), sem("rstd_out"), sem("bn_out")
        act_out, hi0_out, hi1_out, lo_out = sem("act_out"), sem("hi0_out"), sem("hi1_out"), sem("lo_out")
        conv_mm, stats_out, z0_out = sem("conv_mm"), sem("stats_out"), sem("z0_out")
        yc_out, pre_out, xc_out = sem("yc_out"), sem("pre_out"), sem("xc_out")
        yt_mm, yt_out = sem("yt_mm"), sem("yt_out")
        gram_mm, cov_out, rep_mm = sem("gram_mm"), sem("cov_out"), sem("rep_mm")
        sum_mm = sem("sum_mm")
        piv_in, piv_out = sem("piv_in"), sem("piv_out")
        fw_out, fin_mm, stored = sem("fw_out"), sem("fin_mm"), sem("stored")
        bias_mm, bias_out = sem("bias_mm"), sem("bias_out")
        res_act, res_dve = sem("res_act"), sem("res_dve")
        ones_set, dmean_out, warm_set = sem("ones_set"), sem("dmean_out"), sem("warm_set")

        block = ctx.enter_context(nc.Block())

        def x_of(i):
            lay, b = divmod(i, PAIRS)
            return xs[lay][:, b * N:(b + 1) * N]

        def wait_x(eng, i):
            if i < PAIRS:
                eng.wait_ge(x_in[i], 16)
            else:
                eng.wait_ge(x_out, i - PAIRS + 1)

        def lanes(g):
            return slice(g * C, (g + 1) * C)

        def quarter(q):
            return slice(q * N, (q + 1) * N)

        def padded(t, rows, q):
            return t[rows, q, 1:H + 1, 1:W + 1]

        def img(ap):
            return ap.rearrange("p (r w) -> p r w", r=H)

        @block.sync
        def _(sp):
            sp.dma_start(xs[0][:, quarter(0)], x[:, quarter(0)]).then_inc(x_in[0], 16)
            sp.dma_start(prm[:], params).then_inc(prm_in, 16)
            sp.dma_start(aw[:, A_V0:A_Q1], attn_w[:, A_V0:A_Q1]).then_inc(vo0_in, 16)
            sp.dma_start(xs[0][:, quarter(1)], x[:, quarter(1)]).then_inc(x_in[1], 16)
            sp.dma_start(kst[:, 0:K_FIRST], consts[:, 0:K_FIRST]).then_inc(id_in, 16)
            sp.dma_start(sel[:], select).then_inc(sel_in, 16)
            for b in range(2, PAIRS):
                sp.dma_start(xs[0][:, quarter(b)], x[:, quarter(b)]).then_inc(x_in[b], 16)
            sp.dma_start(aw[:, A_Q1:], attn_w[:, A_Q1:]).then_inc(aw1_in, 16)
            for n in range(2):
                sp.dma_start(cw[n][:], conv_w[n].rearrange("p (t c) -> p t c", t=TAPS)).then_inc(cw_in[n], 16)
            sp.dma_start(kst[:, K_FIRST:], consts[:, K_FIRST:]).then_inc(kst_in, 16)
            for k in range(PAIRS):
                sp.wait_ge((res_act, res_dve)[k % 2], k // 2 + 1)
                sp.dma_start(out[:, quarter(k)], res[:, quarter(k)]).then_inc(stored, 16)
            sp.wait_ge(stored, 16 * PAIRS)

        @block.gpsimd
        def _(pool):
            zeroed = [t[:].rearrange("p b r w -> p (b r w)").bitcast(U32) for t in conv_in[0] + conv_in[1]]
            nc.gpsimd.memset(yt[:, :, :, C:C + 1], 1.0).then_inc(ones_set, 1)
            for i in range(ITERS):
                pool.wait_ge(cut_out, 2 * i + 2)
                if i >= 1:
                    pool.wait_ge(parts_out, i)
                nc.gpsimd.tensor_tensor(rest[:], proj[:, i % 2], cut1[:], ALU.subtract).then_inc(rest_out, 1)
                if i < len(zeroed):
                    nc.gpsimd.memset(zeroed[i], 0).then_inc(pads_set, 1)
            for n in range(2):
                pool.wait_ge(sign_out, n + 1)
                pool.wait_ge(pow2_out, n + 1)
                nc.gpsimd.tensor_scalar(taps[n][:], sign[n][:], bn_t[n][:, 2:3], 1.0,
                                        ALU.mult, ALU.mult).then_inc(taps_out, 1)
            pool.wait_ge(id_in, 16)
            mh = kst[:, K_MH:K_MH + 1]
            for n in range(2):
                pool.wait_ge(var_out, n + 1)
                nc.gpsimd.tensor_tensor(rstd[n][:], var[n][:], mh, ALU.pow).then_inc(rstd_out, 1)
            pool.wait_ge(piv_in, 1)
            nc.gpsimd.tensor_tensor(piv[:], dpiv[:], mh, ALU.pow).then_inc(piv_out, 1)

        @block.scalar
        def _(act):
            act.dma_start(aw[:, A_Q0:A_V0], attn_w[:, A_Q0:A_V0]).then_inc(qk0_in, 16)
            nc.scalar.preload_act_table_set("natural_log_exp_and_others")
            act.wait_ge(prm_in, 16)

            def value_weights():
                act.wait_ge(wv0_mm, 1)
                nc.scalar.activation(wv0[:], pb_e[:, 0:P], ACT.Identity,
                                     scale=prm[:, P_GAMMA:P_GAMMA + 1]).then_inc(wv0_set, 1)

            def project_out(i):
                act.wait_ge(qk_mm, i + 1)
                if i >= 2:
                    act.wait_ge(parts_out, i - 1)
                bq, bk = (P_BQ0, P_BK0) if i < PAIRS else (P_BQ1, P_BK1)
                for o, bias in enumerate((bq, bk)):
                    nc.scalar.activation(proj[:, i % 2, o, :], pb_qk[:, o * N:(o + 1) * N], ACT.Identity,
                                         bias=prm[:, bias:bias + 1]).then_inc(qk_out, 1)

            def totals(i, g):
                if i >= 2:
                    act.wait_ge(shift_out, i - 1)
                act.wait_ge(max_out, 2 * i + g + 1)
                for t in range(CH):
                    n = g * CH + t
                    nc.scalar.activation(junk[:, n, :], pb_s[(2 * i + g) % 3][:, t * N:(t + 1) * N], ACT.Exp,
                                         bias=negmax[:, i % 2, n:n + 1],
                                         accum_out=total[:, i % 2, n:n + 1]).then_inc(total_out, 1)
                if g == 1:
                    act.wait_ge(total_out, 4 * i + 4)
                    nc.scalar.activation(lntot[:, i % 2, :], total[:, i % 2, :], ACT.Ln).then_inc(ln_out, 1)

            def exps(i):
                if i >= 2:
                    act.wait_ge(pv_mm, i - 1)
                for g in range(G):
                    act.wait_ge(t_mm, 2 * i + g + 1)
                    nc.scalar.activation(probs[:, i % 2, g], pb_t[g][:].rearrange("p (t n) -> p t n", t=CH),
                                         ACT.Exp).then_inc(exp_out, 1)

            def values_out(i):
                act.wait_ge(v_mm, i + 1)
                if i >= 2:
                    act.wait_ge(pv_mm, i - 1)
                nc.scalar.activation(vt[:, i % 2], pb_v[:, 0:CH * P].rearrange("p (t c) -> p t c", t=CH),
                                     ACT.Identity).then_inc(v_out, 1)

            def shift_rows(i):
                act.wait_ge(rows_mm, i + 1)
                if i >= 2:
                    act.wait_ge(t_mm, 2 * (i - 1))
                nc.scalar.activation(shift_t[:, i % 2, :], pb_shift[0:SHIFTS],
                                     ACT.Identity).then_inc(rows_out, 1)

            for i in range(-3, ITERS):
                if 0 <= i + 1 < ITERS:
                    totals(i + 1, 0)
                if i >= 0:
                    shift_rows(i)
                if 0 <= i + 1 < ITERS:
                    values_out(i + 1)
                if i >= ITERS - 2:
                    n = i - (ITERS - 2)
                    act.wait_ge(cw_in[n], 16)
                    nc.scalar.activation(sign[n][:], cw[n][:], ACT.Sign).then_inc(sign_out, 1)
                if i + 3 < ITERS:
                    project_out(i + 3)
                if i >= 0:
                    exps(i)
                if 0 <= i + 1 < ITERS:
                    totals(i + 1, 1)
                if i == -3:
                    value_weights()
            for n in range(2):
                if n == 1:
                    act.wait_ge(stats_out, 1)
                    nc.scalar.activation(z0[:], pb_conv[0][0][:, 0:N], ACT.Identity).then_inc(z0_out, 1)
                act.wait_ge(bn_out, n + 1)
                for q in range(PAIRS):
                    src = xs[LAYERS][:, quarter(q)] if n == 0 else pb_conv[0][q][:, 0:N]
                    if n == 1 and q == 0:
                        act.wait_ge(z0_out, 1)
                        src = z0[:]
                    if n == 1:
                        act.wait_ge(lo_out, 2 * q + 2)
                    if q == 0:
                        act.wait_ge(pads_set, 4)
                        rows = lanes(0)
                        nc.scalar.activation(padded(conv_in[n][0], rows, q), img(src[rows]), ACT.Relu,
                                             scale=bn_s[n][rows], bias=bn_b[n][rows]).then_inc(hi0_out, 1)
                    else:
                        nc.scalar.activation(act32[:, quarter(q)], src, ACT.Relu, scale=bn_s[n][:],
                                             bias=bn_b[n][:]).then_inc(act_out, 1)
                    rows = lanes(1)
                    nc.scalar.activation(padded(conv_in[n][1], rows, q), img(src[rows]), ACT.Relu,
                                         scale=bn_s[n][rows], bias=bn_b[n][rows]).then_inc(hi1_out, 1)
            act.wait_ge(comb_mm, 3)
            nc.scalar.activation(npre[:], pb_small[:, 0:1], ACT.Identity, scale=-1.0).then_inc(pre_out, 1)
            act.wait_ge(pre_out, 1)
            for q in range(1, PAIRS):
                nc.scalar.activation(xc[:, quarter(q)], xs[LAYERS][:, quarter(q)], ACT.Identity,
                                     bias=npre[:]).then_inc(xc_out, 1)
            act.wait_ge(ones_set, 1)
            for q in range(PAIRS):
                act.wait_ge(yt_mm, q + 1)
                nc.scalar.activation(yt[:, 2 * q:2 * q + 2, :, 0:C],
                                     pb_yt[q % 2][:, 0:2 * P].rearrange("p (k g c) -> p k g c", k=2, g=G),
                                     ACT.Identity).then_inc(yt_out, 1)
            act.wait_ge(bias_out, 1)
            for q in range(0, PAIRS, 2):
                act.wait_ge(fin_mm, q + 1)
                nc.scalar.activation(res[:, quarter(q)], pb_out[q][:, 0:N], ACT.Identity,
                                     bias=bias3[:]).then_inc(res_act, 1)

        @block.tensor
        def _(pe):
            mm = nc.tensor.matmul
            ident = kst[:, K_ID:K_ID + P]
            def value_weights():
                pe.wait_ge(vo0_in, 16)
                pe.wait_ge(prm_in, 16)
                mm(pb_e[:, 0:P], aw[0:C, A_V0:A_V0 + P], aw[0:C, A_O0:A_O0 + P], start=True, stop=True)
                mm(pb_e[:, P:P + 1], aw[0:C, A_O0:A_O0 + P], prm[0:C, P_BV0:P_BV0 + 1],
                   start=True, stop=True).then_inc(wv0_mm, 1)

            def keep_warm(count, bank=pb_warm):
                for _ in range(count):
                    mm(bank[:], warm[:, 0:P], warm[:], start=True, stop=True)

            def project(i, parts):
                wait_x(pe, i)
                if i >= 1:
                    pe.wait_ge(qk_out, 2 * i)
                if i in (0, PAIRS):
                    pe.wait_ge(qk0_in if i == 0 else aw1_in, 16)
                for o in parts:
                    w = ((A_Q0, A_K0) if i < PAIRS else (A_Q1, A_K1))[o]
                    last = mm(pb_qk[:, o * N:(o + 1) * N], aw[:, w:w + P], x_of(i), start=True, stop=True)
                if 1 in parts:
                    last.then_inc(qk_mm, 1)

            def values(i):
                if i >= PAIRS:
                    wait_x(pe, i)
                if i >= 1:
                    pe.wait_ge(v_out, i)
                if i >= 2:
                    pe.wait_ge(rows_out, i - 1)
                if i == 0:
                    pe.wait_ge(wv0_set, 1)
                wv = wv0[:] if i < PAIRS else aw[:, A_V1:A_V1 + P]
                for t in range(CH):
                    last = mm(pb_v[:, t * P:(t + 1) * P], x_of(i)[:, t * P:(t + 1) * P], wv,
                              start=True, stop=True)
                last.then_inc(v_mm, 1)

            def scores(i):
                pe.wait_ge(parts_out, i + 1)
                for g in range(G):
                    unit = 2 * i + g
                    if unit >= 3:
                        pe.wait_ge(total_out, CH * (unit - 2))
                    if i == 0 and g == 0:
                        pe.wait_ge(const0_set, 1)
                    rows = slice(C * g, C * (g + 1))
                    for t in range(CH):
                        last = mm(pb_s[unit % 3][:, t * N:(t + 1) * N], qk[rows, i % DEPTH, 0, t * P:(t + 1) * P],
                                  qk[rows, i % DEPTH, 1, :], start=True, stop=True)
                    last.then_inc(s_mm, 1)

            def scores_t(i):
                pe.wait_ge(rows_out, i + 1)
                if i == 0:
                    pe.wait_ge(sel_set, 1)
                for g in range(G):
                    if i >= 1:
                        pe.wait_ge(exp_out, 2 * i - 1 + g)
                    rows = slice(C * g, C * (g + 1))
                    for t in range(CH):
                        mm(pb_t[g][:, t * N:(t + 1) * N], qk[rows, i % DEPTH, 1, t * P:(t + 1) * P],
                           qk[rows, i % DEPTH, 0, :], start=True, stop=True, skip_group_check=True)
                        for u in range(CH):
                            col = t * N + u * P
                            last = mm(pb_t[g][:, col:col + P], sel16[:, g * CH + u, :], shift_t[:, i % 2, :],
                                      start=False, stop=True, skip_group_check=True)
                    last.then_inc(t_mm, 1)

            def shifts_to_rows(i):
                pe.wait_ge(shift_out, i + 1)
                if i == 0:
                    pe.wait_ge(id16_set, 1)
                nc.tensor.transpose(pb_shift[0:SHIFTS],
                                    shift_p[:, i % 2].rearrange("p s n -> p (s n)"),
                                    ident16[:]).then_inc(rows_mm, 1)

            def mix(i):
                pe.wait_ge(v_out, i + 1)
                if i >= 1:
                    pe.wait_ge(x_out, i)
                for g in range(G):
                    pe.wait_ge(exp_out, 2 * i + g + 1)
                    for t in range(CH):
                        last = mm(pb_pv[g * C:(g + 1) * C, 0:N], vt[:, i % 2, t, g * C:(g + 1) * C],
                                  probs[:, i % 2, g, t, :], start=(t == 0), stop=(t == CH - 1))
                last.then_inc(pv_mm, 1)

            pe.wait_ge(warm_set, 1)
            keep_warm(WARM_START[0], pb_pv)
            for i in range(-3, ITERS):
                if i + 3 < ITERS:
                    project(i + 3, (0, 1) if i < 0 else (0,))
                if i == -3:
                    value_weights()
                if i < 0:
                    keep_warm(WARM_START[i + 4], pb_pv)
                if i + 3 >= ITERS:
                    pe.wait_ge(qk_out, 2 * ITERS)
                    keep_warm(WARM_ATTENTION[0], pb_qk)
                if i >= 0:
                    shifts_to_rows(i)
                    if i + 3 < ITERS:
                        project(i + 3, (1,))
                    else:
                        keep_warm(WARM_ATTENTION[1], pb_qk)
                    scores_t(i)
                if 0 <= i + 2 < ITERS:
                    scores(i + 2)
                if i >= 0:
                    if i + 3 >= ITERS:
                        keep_warm(WARM_ATTENTION[2], pb_qk)
                    mix(i)
                if 0 <= i + 2 < ITERS:
                    values(i + 2)

            def combine(n):
                mm(pb_small[:, 0:2], kst[:, K_AVG:K_AVG + P], mv[n][:], start=True, stop=True)
                mm(pb_small[:, 2:3], kst[:, K_DIF:K_DIF + P], mv[n][:, 0:1], start=True,
                   stop=True).then_inc(comb_mm, 1)

            def conv_taps(n, q, some):
                for k in some:
                    dy, dx = divmod(k, 3)
                    for g in range(G):
                        last = mm(img(pb_conv[n][q][lanes(g), 0:N]), taps[n][:, k, :],
                                  conv_in[n][g][:, q, dy:dy + H, dx:dx + W],
                                  start=(k == 0), stop=(k == TAPS - 1))
                if k == TAPS - 1:
                    last.then_inc(conv_mm, 1)

            def conv(n, q):
                pe.wait_ge(lo_out, 2 * (n * PAIRS + q + 1))
                conv_taps(n, q, range(TAPS))

            def transposed(q):
                pe.wait_ge(yc_out, q + 1)
                if q >= 2:
                    pe.wait_ge(yt_out, q - 1)
                for k in range(2):
                    col = (2 * q + k) * P
                    last = nc.tensor.transpose(pb_yt[q % 2][:, k * P:(k + 1) * P], yc[:, col:col + P], ident)
                last.then_inc(yt_mm, 1)

            def gram(q):
                pe.wait_ge(yt_out, q + 1)
                for k in range(2 * q, 2 * q + 2):
                    for g in range(G):
                        last = mm(pb_gram[0:C, 0:C + 1], yt[:, k, g, 0:C], yt[:, k, g, :], start=False,
                                  stop=(q == PAIRS - 1 and k == 2 * q + 1 and g == G - 1))
                if q == PAIRS - 1:
                    last.then_inc(gram_mm, 1)

            keep_warm(WARM[0], pb_qk)
            pe.wait_ge(bn_v, 1)
            pe.wait_ge(x_out, ITERS)
            combine(0)
            pe.wait_ge(wabs_out, 2)
            for n in range(2):
                last = mm(pb_mean[:, n:n + 1], kst[:, K_ONES:K_ONES + P], wabs[n][:],
                          start=True, stop=True)
            last.then_inc(e_mm, 1)
            keep_warm(WARM[1], pb_qk)
            pe.wait_ge(taps_out, 2)
            for q in range(PAIRS):
                conv(0, q)
            keep_warm(WARM[2])
            pe.wait_ge(bn_v, 2)
            combine(1)
            keep_warm(WARM[3])
            conv(1, 0)
            conv(1, 1)
            pe.wait_ge(bn_v, 3)
            mm(pb_small[:, 0:1], kst[:, K_AVG:K_AVG + P], mv[2][:, 0:1], start=True, stop=True).then_inc(comb_mm, 1)
            conv(1, 2)
            mm(pb_gram[0:C, 0:C + 1], kst[0:C, K_ID:K_ID + C], kst[0:C, K_EPSN:K_EPSN + C + 1],
               start=True, stop=False)
            pe.wait_ge(lo_out, 4 * PAIRS)
            conv_taps(1, PAIRS - 1, range(0, 4))
            transposed(0)
            conv_taps(1, PAIRS - 1, range(4, TAPS))
            transposed(1)
            gram(0)
            transposed(2)
            gram(1)
            transposed(3)
            gram(2)
            gram(3)
            keep_warm(WARM[4])
            pe.wait_ge(cov_out, 2)
            mm(pb_small[:, R_COL:R_COL + Q * (Q + 1)], kst[0:C, K_REP:K_REP + P],
               cov_q[:].rearrange("p i r -> p (i r)"), start=True, stop=True).then_inc(rep_mm, 1)
            mm(pb_bias[:, 0:1], kst[0:C, K_AVG:K_AVG + P], cov[:, Q:Q + 1], start=True, stop=True).then_inc(sum_mm, 1)
            keep_warm(WARM[5])
            pe.wait_ge(fw_out, 1)
            pe.wait_ge(dmean_out, 1)
            mix_w = final_w[:].rearrange("p g q j -> p (g q j)")
            mm(pb_bias[:, 1:2], mix_w, dmean[:], start=True, stop=True).then_inc(bias_mm, 1)
            for q in range(PAIRS):
                mm(pb_out[q][:, 0:N], mix_w, yc[:, quarter(q)], start=True, stop=True).then_inc(fin_mm, 1)

        @block.vector
        def _(dve):
            ve = nc.vector
            steps = [0]

            def step(ins):
                ins.then_inc(dve_step, 1)
                steps[0] += 1
                dve.wait_ge(dve_step, steps[0])

            ve.memset(warm[:].bitcast(U32), 0).then_inc(warm_set, 1)
            dve.wait_ge(prm_in, 16)

            def power_of_two(n):
                t, col = bn_t[n], (P_BNG0, P_BNG1)[n]
                step(ve.tensor_reduce(t[:, 0:1], prm[:, col:col + 2], AX.X, ALU.max, apply_absolute_value=True))
                step(ve.tensor_scalar(t[:, 1:2], t[:, 0:1], 1e-30, 1.0 / FP16_ROOM, ALU.max, ALU.mult))
                step(ve.tensor_scalar(t[:, 2:3].bitcast(U32), t[:, 1:2].bitcast(U32), 0x7F800000, None,
                                      ALU.bitwise_and))
                ve.reciprocal(t[:, 3:4], t[:, 2:3]).then_inc(pow2_out, 1)
                dve.wait_ge(pow2_out, n + 1)
                step(ve.tensor_scalar(t[:, 4:6], prm[:, col:col + 2], t[:, 3:4], None, ALU.mult))

            def layer_constants():
                dve.wait_ge(wv0_set, 1)
                ve.tensor_scalar(const0[:], pb_e[:, P:P + 1], prm[:, P_BO:P_BO + 1],
                                 prm[:, P_GAMMA:P_GAMMA + 1], ALU.add, ALU.mult).then_inc(const0_set, 1)
                dve.wait_ge(id_in, 16)
                ve.tensor_copy(ident16[:], kst[:, K_ID:K_ID + P]).then_inc(id16_set, 1)
                dve.wait_ge(sel_in, 16)
                ve.tensor_copy(sel16[:], sel[:]).then_inc(sel_set, 1)

            def weight_sum(n):
                dve.wait_ge(cw_in[n], 16)
                ve.tensor_reduce(wabs[n][:], cw[n][:], AX.XY, ALU.add,
                                 apply_absolute_value=True).then_inc(wabs_out, 1)

            def maxima(i, g):
                if i >= 2:
                    dve.wait_ge(shift_out, i - 1)
                dve.wait_ge(s_mm, 2 * i + g + 1)
                ve.tensor_reduce(negmax[:, i % 2, g * CH:(g + 1) * CH],
                                 pb_s[(2 * i + g) % 3][:].rearrange("p (t n) -> p t n", t=CH),
                                 AX.X, ALU.max, negate=True).then_inc(max_out, 1)

            def cut_first(i):
                dve.wait_ge(qk_out, 2 * i + 2)
                if i >= 1:
                    dve.wait_ge(rest_out, i)
                for o, m in enumerate((P_MQ1, P_MK1)):
                    ve.tensor_scalar(cut1[:, o], proj[:, i % 2, o], prm[:, m:m + 1], None,
                                     ALU.mult).then_inc(cut_out, 1)

            def cut_second(i):
                dve.wait_ge(rest_out, i + 1)
                for o, m in enumerate((P_MQ2, P_MK2)):
                    last = ve.tensor_scalar(cut2[:, o], rest[:, o], prm[:, m:m + 1], None, ALU.mult)
                step(last)
                if i >= DEPTH:
                    dve.wait_ge(t_mm, 2 * (i - DEPTH + 1))
                ve.tensor_tensor(qk[:, i % DEPTH], rest[:], cut2[:], ALU.subtract).then_inc(parts_out, 1)

            def shifts(i):
                dve.wait_ge(ln_out, i + 1)
                if i >= 2:
                    dve.wait_ge(rows_mm, i - 1)
                p = shift_p[:, i % 2]
                ve.tensor_tensor(shift[:], negmax[:, i % 2, :], lntot[:, i % 2, :], ALU.subtract)
                step(ve.tensor_tensor(p[:, 0, :], negmax[:, i % 2, :], lntot[:, i % 2, :], ALU.subtract))
                ve.tensor_tensor(shift_r[:], shift[:], p[:, 0, :], ALU.subtract)
                step(ve.tensor_tensor(p[:, 1, :], shift[:], p[:, 0, :], ALU.subtract))
                ve.tensor_tensor(p[:, 2, :], shift_r[:], p[:, 1, :], ALU.subtract).then_inc(shift_out, 1)

            def add_shortcut(i):
                lay, b = divmod(i, PAIRS)
                dve.wait_ge(pv_mm, i + 1)
                const = const0[:] if lay == 0 else prm[:, P_BV1:P_BV1 + 1]
                cols = slice(b * N, (b + 1) * N)
                ve.scalar_tensor_tensor(xs[lay + 1][:, cols], pb_pv[:, 0:N], const, xs[lay][:, cols],
                                        ALU.add, ALU.add).then_inc(x_out, 1)
            def statistics(i):
                b = i - PAIRS
                dve.wait_ge(x_out, i + 1)
                step(ve.bn_stats(stats[0][:, 6 * b:6 * b + 6], xs[LAYERS][:, b * N:(b + 1) * N]))

            for i in range(-3, ITERS + 1):
                if 1 <= i <= PAIRS:
                    add_shortcut(i - 1)
                if 0 <= i < ITERS:
                    shifts(i)
                if i > PAIRS:
                    add_shortcut(i - 1)
                if 0 <= i + 2 < ITERS:
                    cut_second(i + 2)
                if 0 <= i + 1 < ITERS:
                    maxima(i + 1, 1)
                if i + 3 < ITERS:
                    cut_first(i + 3)
                if 0 <= i + 2 < ITERS:
                    maxima(i + 2, 0)
                if i > PAIRS:
                    statistics(i - 1)
                if i == -3:
                    layer_constants()
                if i == ITERS - 1:
                    ve.tensor_copy(tt[:, :, Q:2 * Q],
                                   prm[:, P_W3:P_W3 + Q * Q].rearrange("p (i r) -> p i r", i=Q)).then_inc(w3_set, 1)
                if i in (ITERS - 2, ITERS - 1):
                    weight_sum(i - (ITERS - 2))
                    power_of_two(i - (ITERS - 2))

            dve.wait_ge(kst_in, 16)
            def parts(n, q):
                if q == 0:
                    dve.wait_ge(bn_out, n + 1)
                    src = xs[LAYERS][:, quarter(0)] if n == 0 else z0[:]
                    if n == 1:
                        dve.wait_ge(z0_out, 1)
                    step(ve.tensor_scalar(act32[:, quarter(0)], src, bn_s[n][:], bn_b[n][:], ALU.mult, ALU.add))
                    step(ve.tensor_scalar(act32[:, quarter(0)], act32[:, quarter(0)], 0.0, None, ALU.max))
                else:
                    dve.wait_ge(act_out, n * (PAIRS - 1) + q)
                    ve.tensor_copy(padded(conv_in[n][0], lanes(0), q),
                                   img(act32[lanes(0), quarter(q)])).then_inc(hi0_out, 1)
                for g, hi_out in enumerate((hi0_out, hi1_out)):
                    dve.wait_ge(hi_out, n * PAIRS + q + 1)
                    ve.tensor_tensor(padded(conv_in[n][g], lanes(1 - g), q),
                                     img(act32[lanes(g), quarter(q)]), padded(conv_in[n][g], lanes(g), q),
                                     ALU.subtract).then_inc(lo_out, 1)

            for n in range(2):
                if n == 1:
                    dve.wait_ge(e_mm, 1)
                    step(ve.tensor_copy(emean[:], pb_mean[:, 0:2]))
                    step(ve.tensor_tensor(esq[:], emean[:, 0:1], emean[:, 0:1], ALU.mult))
                    step(ve.tensor_scalar(esq[:], esq[:], E_SQUARE_MIN, None, ALU.max))
                    step(ve.reciprocal(einv[:], esq[:]))
                    step(ve.tensor_scalar(eps1[:], einv[:], BN_EPS, None, ALU.mult))
                    for q in range(PAIRS):
                        dve.wait_ge(conv_mm, q + 1)
                        ve.bn_stats(stats[1][:, 6 * q:6 * q + 6], pb_conv[0][q][:, 0:N]).then_inc(stats_out, 1)
                        dve.wait_ge(stats_out, q + 1)
                ve.bn_aggr(mv[n][:], stats[n][:]).then_inc(bn_v, 1)
                dve.wait_ge(comb_mm, n + 1)
                t = bn_t[n]
                step(ve.tensor_scalar(var[n][:], pb_small[:, 2:3], pb_small[:, 2:3],
                                      BN_EPS if n == 0 else eps1[:], ALU.mult, ALU.add))
                ve.tensor_tensor(var[n][:], pb_small[:, 1:2], var[n][:], ALU.add).then_inc(var_out, 1)
                dve.wait_ge(rstd_out, n + 1)
                step(ve.tensor_tensor(bn_s[n][:], t[:, 4:5], rstd[n][:], ALU.mult))
                ve.scalar_tensor_tensor(bn_b[n][:], pb_small[:, 0:1], bn_s[n][:], t[:, 5:6], ALU.mult, ALU.subtract,
                                        reverse1=True).then_inc(bn_out, 1)
                dve.wait_ge(pads_set, 4)
                for q in range(PAIRS if n == 0 else PAIRS - 1):
                    parts(n, q)
            first = quarter(0)
            dve.wait_ge(conv_mm, PAIRS + 1)
            step(ve.scalar_tensor_tensor(yc[:, first], pb_conv[1][0][:, 0:N], emean[:, 1:2],
                                         xs[LAYERS][:, first], ALU.mult, ALU.add))
            step(ve.bn_stats(stats[2][:], yc[:, first]))
            ve.bn_aggr(mv[2][:], stats[2][:]).then_inc(bn_v, 1)
            parts(1, PAIRS - 1)
            dve.wait_ge(pre_out, 1)
            ve.tensor_scalar(yc[:, first], yc[:, first], npre[:], None, ALU.add).then_inc(yc_out, 1)
            for q in range(1, PAIRS):
                dve.wait_ge(conv_mm, PAIRS + q + 1)
                dve.wait_ge(xc_out, q)
                ve.scalar_tensor_tensor(yc[:, quarter(q)], pb_conv[1][q][:, 0:N], emean[:, 1:2],
                                        xc[:, quarter(q)], ALU.mult, ALU.add).then_inc(yc_out, 1)
            dve.wait_ge(gram_mm, 1)
            step(ve.tensor_tensor(gmask[:].rearrange("p q j -> p (q j)"), pb_gram[0:C, 0:C],
                                  kst[0:C, K_MASKJ:K_MASKJ + C], ALU.mult))
            ve.tensor_copy(cov[:, Q:Q + 1], pb_gram[0:C, C:C + 1]).then_inc(cov_out, 1)
            step(ve.tensor_reduce(cov[:, 0:Q], gmask[:], AX.X, ALU.add))
            dve.wait_ge(cov_out, 1)
            ve.tensor_tensor(cov_q[:], cov[:].unsqueeze(1).to_broadcast([C, Q, Q + 1]),
                             kst[0:C, K_HOT:K_HOT + Q].unsqueeze(2).to_broadcast([C, Q, Q + 1]),
                             ALU.mult).then_inc(cov_out, 1)
            dve.wait_ge(rep_mm, 1)
            dve.wait_ge(w3_set, 1)
            rep = pb_small[:, R_COL:R_COL + Q * (Q + 1)].rearrange("p (i r) -> p i r", i=Q)
            step(ve.tensor_copy(means[:], rep[:, :, Q]))
            step(ve.tensor_tensor(dd[:], means[:].unsqueeze(2).to_broadcast([P, Q, Q]),
                                  means[:].unsqueeze(1).to_broadcast([P, Q, Q]), ALU.mult))
            step(ve.tensor_tensor(tt[:, :, 0:Q], rep[:, :, 0:Q], dd[:], ALU.subtract))
            for j in range(Q - 1):
                left, rows = Q - 1 - j, 2 * Q - 1 - j
                step(ve.reciprocal(inv[:, j:j + 1], tt[:, j, j:j + 1]))
                col = tt[:, j:j + 1, j + 1:].to_broadcast([P, left, rows])
                lij = tt[:, j, j + 1:Q].unsqueeze(2).to_broadcast([P, left, rows])
                step(ve.scalar_tensor_tensor(upd[:, j + 1:, j + 1:], col, inv[:, j:j + 1], lij,
                                             ALU.mult, ALU.mult))
                step(ve.tensor_tensor(tt[:, j + 1:, j + 1:], tt[:, j + 1:, j + 1:], upd[:, j + 1:, j + 1:],
                                      ALU.subtract))
            hot = kst[:, K_HOT:K_HOT + Q]
            diag = tt[:].rearrange("p i r -> p (i r)")[:, 0:(Q - 1) * (2 * Q + 1) + 1:2 * Q + 1]
            step(ve.tensor_tensor(own[:], diag, hot, ALU.mult))
            ve.tensor_reduce(dpiv[:], own[:], AX.X, ALU.add).then_inc(piv_in, 1)
            step(ve.tensor_tensor(prod[:], tt[:, :, Q:2 * Q].rearrange("p i r -> p r i"),
                                  hot.unsqueeze(1).to_broadcast([P, Q, Q]), ALU.mult))
            step(ve.tensor_reduce(coef[:], prod[:], AX.X, ALU.add))
            dve.wait_ge(sum_mm, 1)
            ve.tensor_scalar(dmean[:], pb_bias[:, 0:1], -2.0 / NTOT, None,
                             ALU.mult).then_inc(dmean_out, 1)
            spread = coef[:].unsqueeze(1).unsqueeze(3).to_broadcast([P, G, Q, CJ])
            step(ve.tensor_tensor(placed[:], kst[:, K_MASKF:K_MASKF + P]
                                  .rearrange("p (g q j) -> p g q j", g=G, q=Q), spread, ALU.mult))
            dve.wait_ge(piv_out, 1)
            ve.tensor_scalar(final_w[:], placed[:], piv[:], None, ALU.mult).then_inc(fw_out, 1)
            dve.wait_ge(bias_mm, 1)
            ve.tensor_scalar(bias3[:], pb_bias[:, 1:2], prm[:, P_BIAS3:P_BIAS3 + 1], None,
                             ALU.add).then_inc(bias_out, 1)
            dve.wait_ge(bias_out, 1)
            for q in range(1, PAIRS, 2):
                dve.wait_ge(fin_mm, q + 1)
                ve.tensor_scalar(res[:, quarter(q)], pb_out[q][:, 0:N], bias3[:], None,
                                 ALU.add).then_inc(res_dve, 1)


def kernel(**inputs):
    import concourse.bacc as bacc
    from concourse.bass_utils import run_bass_kernel_spmd

    a = {name: np.asarray(v) for name, v in inputs.items()}

    def halves(m):
        return np.concatenate([m, m], axis=0)

    def diagonal(m, rows=C):
        out = np.zeros((P, P), m.dtype)
        out[0:m.shape[0], 0:m.shape[1]] = m
        out[rows:rows + m.shape[0], C:C + m.shape[1]] = m
        return out

    x = a["x"].reshape(G, PAIRS, C, N).transpose(0, 2, 1, 3).reshape(P, FREE)

    def groups(m):
        out = np.zeros(m.shape[:-1] + (C,), m.dtype)
        for n in range(len(PARTS)):
            out[..., n * CQ:(n + 1) * CQ] = m
        return out

    attn_w = np.concatenate([
        diagonal(groups(a["L0_conv_Wq"].T)), diagonal(groups(a["L0_conv_Wk"].T)),
        diagonal(a["L0_conv_Wv"], CV), diagonal(a["L0_conv_Wo"].T, CV),
        diagonal(groups(a["L1_conv_Wq"].T)), diagonal(groups(a["L1_conv_Wk"].T)),
        diagonal(a["L1_conv_Wv"].T)], axis=1)
    params = np.zeros((P, P_COLS), np.float32)
    for g in range(G):
        row = g * C
        for lay, (pq, pk) in enumerate(((P_BQ0, P_BK0), (P_BQ1, P_BK1))):
            params[row:row + C, pq] = groups(a[f"L{lay}_conv_bq"])
            params[row:row + C, pk] = groups(a[f"L{lay}_conv_bk"])
        for n, (part_q, part_k) in enumerate(PARTS):
            at = slice(row + n * CQ, row + (n + 1) * CQ)
            params[at, P_MQ1], params[at, P_MQ2] = part_q >= 1, part_q == 2
            params[at, P_MK1], params[at, P_MK2] = part_k >= 1, part_k == 2
        params[g * CV:(g + 1) * CV, P_BV0] = a["L0_conv_bv"]
    params[:, P_GAMMA] = a["L0_conv_gamma"][0]
    for col, name in ((P_BO, "L0_conv_bo"), (P_BV1, "L1_conv_bv"), (P_BNG0, "L2_conv_gamma0"),
                      (P_BNB0, "L2_conv_beta0"), (P_BNG1, "L2_conv_gamma1"), (P_BNB1, "L2_conv_beta1")):
        params[:, col] = halves(a[name])
    params[:, P_BIAS3] = halves(a["L3_conv_bias"].reshape(C))
    w3 = a["L3_conv_weight"].transpose(2, 1, 0).reshape(CJ, Q * Q)
    params[:, P_W3:P_W3 + Q * Q] = np.concatenate([w3] * (G * Q), axis=0)
    conv_w = [halves(a[f"L2_conv_w{n}"].reshape(C, C, TAPS).transpose(1, 2, 0).reshape(C, TAPS * C))
              for n in range(2)]

    nc = bacc.Bacc("TRN2", target_bir_lowering=False, num_devices=1)
    arrays = {"x_in": x, "attn_w": attn_w, "params": params, "consts": constants(),
              "select": selectors().reshape(SHIFTS, G * CH * P),
              "conv_w0": conv_w[0], "conv_w1": conv_w[1]}
    arrays = {name: np.ascontiguousarray(v) for name, v in arrays.items()}
    t = {name: nc.dram_tensor(name, v.shape, mybir.dt.from_np(v.dtype), kind="ExternalInput").ap()
         for name, v in arrays.items()}
    out = nc.dram_tensor("out", (P, FREE), F32, kind="ExternalOutput").ap()
    build(nc, t["x_in"], t["attn_w"], t["params"], t["consts"],
          t["select"].rearrange("p (n m) -> p n m", n=G * CH), [t["conv_w0"], t["conv_w1"]], out)
    r = run_bass_kernel_spmd(nc, [arrays], core_ids=[0])
    got = r.results[0]["out"]
    return got.reshape(G, C, PAIRS, N).transpose(0, 2, 1, 3).reshape(B, C, H, W)
```

```python
from contextlib import ExitStack

import concourse.bass as bass
import numpy as np
from concourse import mybir

F32 = mybir.dt.float32
F16 = mybir.dt.float16
BF16 = mybir.dt.bfloat16
U32 = mybir.dt.uint32
ALU = mybir.AluOpType
ACT = mybir.ActivationFunctionType
AX = mybir.AxisListType

P = 128
B, C, H, W = 8, 64, 16, 16
G = 2
PAIRS = B // G
N = H * W
CH = N // P
FREE = PAIRS * N
LAYERS = 2
ITERS = LAYERS * PAIRS
CQ = C // 8
CV = C // 2
PARTS = ((0, 0), (0, 1), (1, 0), (1, 1), (0, 2), (2, 0), (1, 2), (2, 1))
SPLIT = 3
DEPTH = 4
DVE_RESTS, DVE_PARTS = 1, 2
TAPS = 9
WP = W + 2
HALF = 512
Q = 4
CJ = C // Q
NTOT = B * N
BN_EPS = 1e-5
WARM = (4, 13, 2, 14, 3, 15)
WARM_START = (6, 2, 3, 3)
WARM_ATTENTION = (1, 2, 6, 2)
E_SQUARE_MIN = 1e-37
FP16_ROOM = 128.0

(P_BQ0, P_BK0, P_BQ1, P_BK1, P_GAMMA, P_BO, P_BV0, P_BV1, P_BNG0, P_BNB0, P_BNG1, P_BNB1,
 P_BIAS3, P_MQ1, P_MQ2, P_MK1, P_MK2) = range(17)
P_W3 = 17
P_COLS = P_W3 + Q * Q

K_ID = 0
K_MH = K_ID + P
K_FIRST = K_MH + 1
K_AVG = K_FIRST
K_DIF = K_AVG + P
K_REP = K_DIF + P
K_ONES = K_REP + P
K_MASKJ = K_ONES + P
K_MASKF = K_MASKJ + C
K_HOT = K_MASKF + P
K_EPSN = K_HOT + Q
K_COLS = K_EPSN + C + 1
SHIFTS = SPLIT * G * CH

A_Q0, A_K0, A_V0, A_O0, A_Q1, A_K1, A_V1 = (P * n for n in range(7))
A_COLS = 7 * P


def constants():
    part = np.arange(P)
    same_c = part[:, None] % C == part[None, :] % C
    same_g = part[:, None] // C == part[None, :] // C
    k = np.zeros((P, K_COLS), np.float32)
    k[:, K_ID:K_ID + P] = np.eye(P)
    k[:, K_AVG:K_AVG + P] = 0.5 * same_c
    k[:, K_DIF:K_DIF + P] = np.where(same_c, np.where(same_g, 0.5, -0.5), 0)
    k[:C, K_REP:K_REP + P] = (part[:C, None] % CJ == part[None, :] % CJ) / NTOT
    k[:, K_ONES:K_ONES + P] = 1.0 / (P * C * TAPS)
    k[:, K_MASKJ:K_MASKJ + C] = part[:, None] % CJ == part[None, :C] % CJ
    k[:, K_MASKF:K_MASKF + P] = same_g & (part[:, None] % CJ == part[None, :] % CJ)
    k[:, K_HOT:K_HOT + Q] = (part[:, None] % C) // CJ == np.arange(Q)
    k[:C, K_EPSN:K_EPSN + C] = BN_EPS * NTOT * np.eye(C)
    k[:, K_MH] = -0.5
    return k


def selectors():
    rows = np.arange(SHIFTS)[:, None, None] % (G * CH)
    return np.broadcast_to(rows == np.arange(G * CH)[None, :, None], (SHIFTS, G * CH, P)).astype(np.float32)


def build(nc, x, attn_w, params, consts, select, conv_w, out):
    with ExitStack() as ctx:
        def sb(name, shape, dt=F32):
            return ctx.enter_context(nc.sbuf_tensor(name, shape, dt))

        def sem(name):
            return ctx.enter_context(nc.semaphore(name))

        xs = [sb(f"x{n}", [P, FREE]) for n in range(LAYERS + 1)]
        aw = sb("aw", [P, A_COLS])
        prm = sb("prm", [P, P_COLS])
        kst = sb("kst", [P, K_COLS])
        sel = sb("sel", [SHIFTS, G * CH, P])
        cw = [sb(f"cw{n}", [P, TAPS, C]) for n in range(2)]
        wv0 = sb("wv0", [P, P])
        const0 = sb("const0", [P, 1])
        proj = sb("proj", [P, 2, 2, N])
        cut1 = sb("cut1", [P, 2, N], BF16)
        rest = sb("rest", [P, 2, N])
        cut2 = sb("cut2", [P, 2, N], BF16)
        qk = sb("qk", [P, DEPTH, 2, N], BF16)
        vt = sb("vt", [P, 2, CH, P])
        negmax = sb("negmax", [P, 2, G * CH])
        junk = sb("junk", [P, G * CH, N], BF16)
        total = sb("total", [P, 2, G * CH])
        lntot = sb("lntot", [P, 2, G * CH])
        shift = sb("shift", [P, G * CH])
        shift_r = sb("shift_r", [P, G * CH])
        shift_p = sb("shift_p", [P, 2, SPLIT, G * CH], BF16)
        shift_t = sb("shift_t", [SHIFTS, 2, P], BF16)
        sel16 = sb("sel16", [SHIFTS, G * CH, P], BF16)
        probs = sb("probs", [P, 2, G, CH, N])
        ident16 = sb("ident16", [P, P], BF16)
        stats = [sb(f"stats{n}", [P, 6 * k]) for n, k in ((0, PAIRS), (1, PAIRS), (2, 1))]
        mv = [sb(f"mv{n}", [P, 2]) for n in range(3)]
        npre = sb("npre", [P, 1])
        var = [sb(f"var{n}", [P, 1]) for n in range(2)]
        rstd = [sb(f"rstd{n}", [P, 1]) for n in range(2)]
        bn_s = [sb(f"bn_s{n}", [P, 1]) for n in range(2)]
        bn_b = [sb(f"bn_b{n}", [P, 1]) for n in range(2)]
        bn_t = [sb(f"bn_t{n}", [P, 8]) for n in range(2)]
        sign = [sb(f"sign{n}", [P, TAPS, C]) for n in range(2)]
        taps = [sb(f"taps{n}", [P, TAPS, C], BF16) for n in range(2)]
        wabs = [sb(f"wabs{n}", [P, 1]) for n in range(2)]
        esq, einv, eps1 = (sb(name, [P, 1]) for name in ("esq", "einv", "eps1"))
        emean = sb("emean", [P, 2])
        z0 = sb("z0", [P, N])
        act32 = sb("act32", [P, FREE])
        conv_in = [[sb(f"conv_in{n}{g}", [P, PAIRS, H + 2, WP], F16) for g in range(G)] for n in range(2)]
        xc = sb("xc", [P, FREE])
        yc = sb("yc", [P, FREE])
        warm = sb("warm", [P, HALF], BF16)
        yt = sb("yt", [P, FREE // P, G, C + 1])
        gmask = sb("gmask", [C, Q, CJ])
        cov = sb("cov", [C, Q + 1])
        cov_q = sb("cov_q", [C, Q, Q + 1])
        dmean = sb("dmean", [P, 1])
        means = sb("means", [P, Q])
        dd = sb("dd", [P, Q, Q])
        own = sb("own", [P, Q])
        bias3 = sb("bias3", [P, 1])
        tt = sb("tt", [P, Q, 2 * Q])
        upd = sb("upd", [P, Q, 2 * Q])
        inv = sb("inv", [P, Q - 1])
        dpiv = sb("dpiv", [P, 1])
        piv = sb("piv", [P, 1])
        prod = sb("prod", [P, Q, Q])
        coef = sb("coef", [P, Q])
        placed = sb("placed", [P, G, Q, CJ])
        final_w = sb("final_w", [P, G, Q, CJ])
        res = sb("res", [P, FREE])

        banks = [ctx.enter_context(nc.psum_tensor(f"bank{n}", [P, HALF], F32)) for n in range(8)]
        pb_q, pb_v, pb_pv = banks[0], banks[1], banks[3]
        pb_proj = (pb_q[:, 0:N], pb_pv[:, N:2 * N])
        pb_s, pb_t = [banks[n] for n in (2, 4, 5)], banks[6:8]
        pb_shift = pb_v[:].bitcast(BF16)[:, 4 * P:5 * P]
        pb_conv = [[banks[n] for n in ns] for ns in ((0, 1, 4, 5), (6, 7, 2, 0))]
        pb_small = banks[3]
        pb_e = banks[5]
        pb_yt = banks[4:6]
        pb_gram = banks[1]
        pb_out = pb_conv[1]
        pb_warm = banks[6]
        pb_mean = banks[7]
        R_COL = 8
        pb_bias = banks[4]

        x_in = [sem(f"x_in{n}") for n in range(PAIRS)]
        qk0_in, vo0_in, aw1_in = sem("qk0_in"), sem("vo0_in"), sem("aw1_in")
        prm_in, id_in, sel_in, kst_in = sem("prm_in"), sem("id_in"), sem("sel_in"), sem("kst_in")
        cw_in = [sem(f"cw_in{n}") for n in range(2)]
        pads_set = sem("pads_set")
        wv0_mm, wv0_set, const0_set = sem("wv0_mm"), sem("wv0_set"), sem("const0_set")
        qk_mm, qk_out = sem("qk_mm"), sem("qk_out")
        v_mm, v_out = sem("v_mm"), sem("v_out")
        s_mm, max_out = sem("s_mm"), sem("max_out")
        cut2_out, parts_out = sem("cut2_out"), sem("parts_out")
        total_out, ln_out, shift_out = sem("total_out"), sem("ln_out"), sem("shift_out")
        rows_mm, rows_out = sem("rows_mm"), sem("rows_out")
        id16_set, sel_set = sem("id16_set"), sem("sel_set")
        pow2_out = sem("pow2_out")
        cut_out, rest_out = sem("cut_out"), sem("rest_out")
        t_mm, exp_out = sem("t_mm"), sem("exp_out")
        pv_mm, x_out = sem("pv_mm"), sem("x_out")
        dve_step, w3_set = sem("dve_step"), sem("w3_set")
        sign_out, taps_out = sem("sign_out"), sem("taps_out")
        wabs_out, e_mm = sem("wabs_out"), sem("e_mm")
        bn_v = sem("bn_v")
        comb_mm = sem("comb_mm")
        var_out, rstd_out, bn_out = sem("var_out"), sem("rstd_out"), sem("bn_out")
        act_out, hi0_out, hi1_out, lo_out = sem("act_out"), sem("hi0_out"), sem("hi1_out"), sem("lo_out")
        conv_mm, stats_out, z0_out = sem("conv_mm"), sem("stats_out"), sem("z0_out")
        yc_out, pre_out, xc_out = sem("yc_out"), sem("pre_out"), sem("xc_out")
        yt_mm, yt_out = sem("yt_mm"), sem("yt_out")
        gram_mm, cov_out, rep_mm = sem("gram_mm"), sem("cov_out"), sem("rep_mm")
        sum_mm, own_out = sem("sum_mm"), sem("own_out")
        inv_out = sem("inv_out")
        piv_in, piv_out = sem("piv_in"), sem("piv_out")
        fw_out, fin_mm, stored = sem("fw_out"), sem("fin_mm"), sem("stored")
        bias_mm, bias_out = sem("bias_mm"), sem("bias_out")
        res_act, res_dve = sem("res_act"), sem("res_dve")
        ones_set, dmean_out, warm_set = sem("ones_set"), sem("dmean_out"), sem("warm_set")

        hot = kst[:, K_HOT:K_HOT + Q]
        block = ctx.enter_context(nc.Block())

        def x_of(i):
            lay, b = divmod(i, PAIRS)
            return xs[lay][:, b * N:(b + 1) * N]

        def wait_x(eng, i):
            if i < PAIRS:
                eng.wait_ge(x_in[i], 16)
            else:
                eng.wait_ge(x_out, i - PAIRS + 1)

        def mixed(i):
            return pb_pv[:, 0:N] if i < ITERS - 1 else pb_v[:, 0:N]

        def lanes(g):
            return slice(g * C, (g + 1) * C)

        def quarter(q):
            return slice(q * N, (q + 1) * N)

        def padded(t, rows, q):
            return t[rows, q, 1:H + 1, 1:W + 1]

        def img(ap):
            return ap.rearrange("p (r w) -> p r w", r=H)

        @block.sync
        def _(sp):
            sp.dma_start(xs[0][:, quarter(0)], x[:, quarter(0)]).then_inc(x_in[0], 16)
            sp.dma_start(prm[:], params).then_inc(prm_in, 16)
            sp.dma_start(aw[:, A_V0:A_Q1], attn_w[:, A_V0:A_Q1]).then_inc(vo0_in, 16)
            sp.dma_start(xs[0][:, quarter(1)], x[:, quarter(1)]).then_inc(x_in[1], 16)
            sp.dma_start(kst[:, 0:K_FIRST], consts[:, 0:K_FIRST]).then_inc(id_in, 16)
            sp.dma_start(sel[:], select).then_inc(sel_in, 16)
            for b in range(2, PAIRS):
                sp.dma_start(xs[0][:, quarter(b)], x[:, quarter(b)]).then_inc(x_in[b], 16)
            sp.dma_start(aw[:, A_Q1:], attn_w[:, A_Q1:]).then_inc(aw1_in, 16)
            for n in range(2):
                sp.dma_start(cw[n][:], conv_w[n].rearrange("p (t c) -> p t c", t=TAPS)).then_inc(cw_in[n], 16)
            sp.dma_start(kst[:, K_FIRST:], consts[:, K_FIRST:]).then_inc(kst_in, 16)
            for k in range(PAIRS):
                sp.wait_ge((res_act, res_dve)[k % 2], k // 2 + 1)
                sp.dma_start(out[:, quarter(k)], res[:, quarter(k)]).then_inc(stored, 16)
            sp.wait_ge(stored, 16 * PAIRS)

        @block.gpsimd
        def _(pool):
            zeroed = [t[:].rearrange("p b r w -> p (b r w)").bitcast(U32) for t in conv_in[0] + conv_in[1]]
            nc.gpsimd.memset(yt[:, :, :, C:C + 1], 1.0).then_inc(ones_set, 1)

            def own_parts(i):
                if i >= DEPTH:
                    pool.wait_ge(t_mm, 2 * (i - DEPTH + 1))
                for o in range(2):
                    pool.wait_ge(cut2_out, 2 * i + o + 1)
                    nc.gpsimd.tensor_tensor(qk[:, i % DEPTH, o], rest[:, o], cut2[:, o],
                                            ALU.subtract).then_inc(parts_out, 1)

            for i in range(ITERS):
                if i > DVE_PARTS:
                    own_parts(i - 1)
                for o in range(2 if i >= DVE_RESTS else 0):
                    pool.wait_ge(cut_out, 2 * i + o + 1)
                    pool.wait_ge(parts_out, 2 * (i - 1) + o + 1)
                    nc.gpsimd.tensor_tensor(rest[:, o], proj[:, i % 2, o], cut1[:, o],
                                            ALU.subtract).then_inc(rest_out, 1)
                if i < len(zeroed):
                    nc.gpsimd.memset(zeroed[i], 0).then_inc(pads_set, 1)
            own_parts(ITERS - 1)
            pool.wait_ge(id_in, 16)
            mh = kst[:, K_MH:K_MH + 1]
            for n in range(2):
                pool.wait_ge(sign_out, n + 1)
                pool.wait_ge(pow2_out, n + 1)
                nc.gpsimd.tensor_scalar(taps[n][:], sign[n][:], bn_t[n][:, 2:3], 1.0,
                                        ALU.mult, ALU.mult).then_inc(taps_out, 1)
                pool.wait_ge(var_out, n + 1)
                nc.gpsimd.tensor_tensor(rstd[n][:], var[n][:], mh, ALU.pow).then_inc(rstd_out, 1)
            pool.wait_ge(piv_in, 1)
            nc.gpsimd.tensor_tensor(piv[:], dpiv[:], mh, ALU.pow).then_inc(piv_out, 1)

        @block.scalar
        def _(act):
            act.dma_start(aw[:, A_Q0:A_V0], attn_w[:, A_Q0:A_V0]).then_inc(qk0_in, 16)
            nc.scalar.preload_act_table_set("natural_log_exp_and_others")
            act.wait_ge(prm_in, 16)

            def value_weights():
                act.wait_ge(wv0_mm, 1)
                nc.scalar.activation(wv0[:], pb_e[:, 0:P], ACT.Identity,
                                     scale=prm[:, P_GAMMA:P_GAMMA + 1]).then_inc(wv0_set, 1)

            def copies16():
                act.wait_ge(id_in, 16)
                nc.scalar.activation(ident16[:], kst[:, K_ID:K_ID + P], ACT.Identity).then_inc(id16_set, 1)
                act.wait_ge(sel_in, 16)
                nc.scalar.activation(sel16[:], sel[:], ACT.Identity).then_inc(sel_set, 1)

            def project_out(i):
                for o, bias in enumerate((P_BQ0, P_BK0) if i < PAIRS else (P_BQ1, P_BK1)):
                    act.wait_ge(qk_mm, 2 * i + o + 1)
                    if i >= 2:
                        act.wait_ge(rest_out, 2 * (i - 2) + o + 1)
                    nc.scalar.activation(proj[:, i % 2, o, :], pb_proj[o], ACT.Identity,
                                         bias=prm[:, bias:bias + 1]).then_inc(qk_out, 1)

            def totals(i, g):
                if i >= 2:
                    act.wait_ge(shift_out, i - 1)
                act.wait_ge(max_out, 2 * i + g + 1)
                for t in range(CH):
                    n = g * CH + t
                    nc.scalar.activation(junk[:, n, :], pb_s[(2 * i + g) % 3][:, t * N:(t + 1) * N], ACT.Exp,
                                         bias=negmax[:, i % 2, n:n + 1],
                                         accum_out=total[:, i % 2, n:n + 1]).then_inc(total_out, 1)
                if g == 1:
                    act.wait_ge(total_out, 4 * i + 4)
                    nc.scalar.activation(lntot[:, i % 2, :], total[:, i % 2, :], ACT.Ln).then_inc(ln_out, 1)

            def exps(i):
                if i >= 2:
                    act.wait_ge(pv_mm, i - 1)
                for g in range(G):
                    act.wait_ge(t_mm, 2 * i + g + 1)
                    nc.scalar.activation(probs[:, i % 2, g], pb_t[g][:].rearrange("p (t n) -> p t n", t=CH),
                                         ACT.Exp).then_inc(exp_out, 1)

            def shift_rows(i):
                act.wait_ge(rows_mm, i + 1)
                if i >= 2:
                    act.wait_ge(t_mm, 2 * (i - 1))
                nc.scalar.activation(shift_t[:, i % 2, :], pb_shift[0:SHIFTS],
                                     ACT.Identity).then_inc(rows_out, 1)

            for i in range(-3, ITERS):
                if 0 <= i + 1 < ITERS:
                    totals(i + 1, 0)
                    totals(i + 1, 1)
                if i + 3 < ITERS:
                    project_out(i + 3)
                if i == -3:
                    value_weights()
                    copies16()
                if i >= 0:
                    exps(i)
                if 0 <= i + 1 < ITERS:
                    shift_rows(i + 1)
                if i in (ITERS - 2, ITERS - 1):
                    n = i - (ITERS - 2)
                    act.wait_ge(cw_in[n], 16)
                    nc.scalar.activation(sign[n][:], cw[n][:], ACT.Sign).then_inc(sign_out, 1)

            for n in range(2):
                if n == 1:
                    act.wait_ge(stats_out, 1)
                    nc.scalar.activation(z0[:], pb_conv[0][0][:, 0:N], ACT.Identity).then_inc(z0_out, 1)
                act.wait_ge(bn_out, n + 1)
                for q in range(PAIRS):
                    src = xs[LAYERS][:, quarter(q)] if n == 0 else pb_conv[0][q][:, 0:N]
                    if n == 1 and q == 0:
                        act.wait_ge(z0_out, 1)
                        src = z0[:]
                    if n == 1:
                        act.wait_ge(lo_out, 2 * q + 2)
                    if q == 0:
                        act.wait_ge(pads_set, 4)
                        rows = lanes(0)
                        nc.scalar.activation(padded(conv_in[n][0], rows, q), img(src[rows]), ACT.Relu,
                                             scale=bn_s[n][rows], bias=bn_b[n][rows]).then_inc(hi0_out, 1)
                    else:
                        nc.scalar.activation(act32[:, quarter(q)], src, ACT.Relu, scale=bn_s[n][:],
                                             bias=bn_b[n][:]).then_inc(act_out, 1)
                    rows = lanes(1)
                    nc.scalar.activation(padded(conv_in[n][1], rows, q), img(src[rows]), ACT.Relu,
                                         scale=bn_s[n][rows], bias=bn_b[n][rows]).then_inc(hi1_out, 1)
            act.wait_ge(comb_mm, 3)
            nc.scalar.activation(npre[:], pb_small[:, 0:1], ACT.Identity, scale=-1.0).then_inc(pre_out, 1)
            act.wait_ge(pre_out, 1)
            for q in range(1, PAIRS):
                nc.scalar.activation(xc[:, quarter(q)], xs[LAYERS][:, quarter(q)], ACT.Identity,
                                     bias=npre[:]).then_inc(xc_out, 1)
            act.wait_ge(ones_set, 1)
            for q in range(PAIRS):
                act.wait_ge(yt_mm, q + 1)
                nc.scalar.activation(yt[:, 2 * q:2 * q + 2, :, 0:C],
                                     pb_yt[q % 2][:, 0:2 * P].rearrange("p (k g c) -> p k g c", k=2, g=G),
                                     ACT.Identity).then_inc(yt_out, 1)
            for j in range(Q - 1):
                act.wait_ge(inv_out, j + 1)
                if j:
                    act.wait_ge(own_out, j)
                nc.scalar.activation(own[:, j + 1:j + 2], tt[:, j, j:j + 1], ACT.Identity, scale=hot[:, j:j + 1],
                                     bias=own[:, j:j + 1] if j else 0.0).then_inc(own_out, 1)
            act.wait_ge(bias_out, 1)
            for q in range(0, PAIRS, 2):
                act.wait_ge(fin_mm, q + 1)
                nc.scalar.activation(res[:, quarter(q)], pb_out[q][:, 0:N], ACT.Identity,
                                     bias=bias3[:]).then_inc(res_act, 1)

        @block.tensor
        def _(pe):
            mm = nc.tensor.matmul
            ident = kst[:, K_ID:K_ID + P]

            def value_weights():
                pe.wait_ge(vo0_in, 16)
                pe.wait_ge(prm_in, 16)
                mm(pb_e[:, 0:P], aw[0:C, A_V0:A_V0 + P], aw[0:C, A_O0:A_O0 + P], start=True, stop=True)
                mm(pb_e[:, P:P + 1], aw[0:C, A_O0:A_O0 + P], prm[0:C, P_BV0:P_BV0 + 1],
                   start=True, stop=True).then_inc(wv0_mm, 1)

            def keep_warm(count, bank=pb_warm):
                for _ in range(count):
                    mm(bank[:], warm[:, 0:P], warm[:], start=True, stop=True)

            def project(i):
                wait_x(pe, i)
                if i >= 1:
                    pe.wait_ge(qk_out, 2 * i)
                if i in (0, PAIRS):
                    pe.wait_ge(qk0_in if i == 0 else aw1_in, 16)
                for o, w in enumerate((A_Q0, A_K0) if i < PAIRS else (A_Q1, A_K1)):
                    mm(pb_proj[o], aw[:, w:w + P], x_of(i), start=True, stop=True).then_inc(qk_mm, 1)

            def values(i):
                if i >= PAIRS:
                    wait_x(pe, i)
                if i >= 1:
                    pe.wait_ge(v_out, i)
                if i >= 2:
                    pe.wait_ge(rows_out, i - 1)
                if i == 0:
                    pe.wait_ge(wv0_set, 1)
                wv = wv0[:] if i < PAIRS else aw[:, A_V1:A_V1 + P]
                for t in range(CH):
                    last = mm(pb_v[:, t * P:(t + 1) * P], x_of(i)[:, t * P:(t + 1) * P], wv,
                              start=True, stop=True)
                last.then_inc(v_mm, 1)

            def scores(i):
                pe.wait_ge(parts_out, 2 * i + 2)
                for g in range(G):
                    unit = 2 * i + g
                    if unit >= 3:
                        pe.wait_ge(total_out, CH * (unit - 2))
                    if unit == 2:
                        pe.wait_ge(const0_set, 1)
                    rows = slice(C * g, C * (g + 1))
                    for t in range(CH):
                        last = mm(pb_s[unit % 3][:, t * N:(t + 1) * N], qk[rows, i % DEPTH, 0, t * P:(t + 1) * P],
                                  qk[rows, i % DEPTH, 1, :], start=True, stop=True)
                    last.then_inc(s_mm, 1)

            def scores_t(i):
                pe.wait_ge(rows_out, i + 1)
                if i == 0:
                    pe.wait_ge(sel_set, 1)
                for g in range(G):
                    if i >= 1:
                        pe.wait_ge(exp_out, 2 * i - 1 + g)
                    rows = slice(C * g, C * (g + 1))
                    for t in range(CH):
                        mm(pb_t[g][:, t * N:(t + 1) * N], qk[rows, i % DEPTH, 1, t * P:(t + 1) * P],
                           qk[rows, i % DEPTH, 0, :], start=True, stop=True, skip_group_check=True)
                        for u in range(CH):
                            col = t * N + u * P
                            last = mm(pb_t[g][:, col:col + P], sel16[:, g * CH + u, :], shift_t[:, i % 2, :],
                                      start=False, stop=True, skip_group_check=True)
                    last.then_inc(t_mm, 1)

            def shifts_to_rows(i):
                pe.wait_ge(shift_out, i + 1)
                pe.wait_ge(v_out, i + 1)
                if i == 0:
                    pe.wait_ge(id16_set, 1)
                nc.tensor.transpose(pb_shift[0:SHIFTS],
                                    shift_p[:, i % 2].rearrange("p s n -> p (s n)"),
                                    ident16[:]).then_inc(rows_mm, 1)

            def mix(i):
                pe.wait_ge(v_out, i + 1)
                if i < ITERS - 1:
                    pe.wait_ge(qk_out, 2 * min(i + 4, ITERS))
                    if i >= 1:
                        pe.wait_ge(x_out, i)
                else:
                    pe.wait_ge(rows_out, ITERS)
                for g in range(G):
                    pe.wait_ge(exp_out, 2 * i + g + 1)
                    for t in range(CH):
                        last = mm(mixed(i)[g * C:(g + 1) * C], vt[:, i % 2, t, g * C:(g + 1) * C],
                                  probs[:, i % 2, g, t, :], start=(t == 0), stop=(t == CH - 1))
                last.then_inc(pv_mm, 1)

            pe.wait_ge(warm_set, 1)
            keep_warm(WARM_START[0], pb_t[0])
            project(0)
            value_weights()
            keep_warm(WARM_START[1], pb_t[0])
            for i in range(2):
                project(i + 1)
                scores(i)
                values(i)
                if i == 1:
                    shifts_to_rows(0)
                keep_warm(WARM_START[i + 2], pb_t[0])
            for i in range(ITERS - 2):
                scores_t(i)
                if i + 3 < ITERS:
                    project(i + 3)
                else:
                    pe.wait_ge(qk_out, 2 * ITERS)
                    keep_warm(WARM_ATTENTION[0], pb_q)
                values(i + 2)
                scores(i + 2)
                shifts_to_rows(i + 1)
                if i + 3 == ITERS:
                    keep_warm(WARM_ATTENTION[1], pb_q)
                mix(i)
            scores_t(ITERS - 2)
            keep_warm(WARM_ATTENTION[2], pb_q)
            shifts_to_rows(ITERS - 1)
            keep_warm(WARM_ATTENTION[3], pb_q)
            scores_t(ITERS - 1)
            mix(ITERS - 2)
            mix(ITERS - 1)

            def combine(n):
                mm(pb_small[:, 0:2], kst[:, K_AVG:K_AVG + P], mv[n][:], start=True, stop=True)
                mm(pb_small[:, 2:3], kst[:, K_DIF:K_DIF + P], mv[n][:, 0:1], start=True,
                   stop=True).then_inc(comb_mm, 1)

            def conv_taps(n, q, some):
                for k in some:
                    dy, dx = divmod(k, 3)
                    for g in range(G):
                        last = mm(img(pb_conv[n][q][lanes(g), 0:N]), taps[n][:, k, :],
                                  conv_in[n][g][:, q, dy:dy + H, dx:dx + W],
                                  start=(k == 0), stop=(k == TAPS - 1))
                if k == TAPS - 1:
                    last.then_inc(conv_mm, 1)

            def conv(n, q):
                pe.wait_ge(lo_out, 2 * (n * PAIRS + q + 1))
                conv_taps(n, q, range(TAPS))

            def transposed(q):
                pe.wait_ge(yc_out, q + 1)
                if q >= 2:
                    pe.wait_ge(yt_out, q - 1)
                for k in range(2):
                    col = (2 * q + k) * P
                    last = nc.tensor.transpose(pb_yt[q % 2][:, k * P:(k + 1) * P], yc[:, col:col + P], ident)
                last.then_inc(yt_mm, 1)

            def gram(q):
                pe.wait_ge(yt_out, q + 1)
                for k in range(2 * q, 2 * q + 2):
                    for g in range(G):
                        last = mm(pb_gram[0:C, 0:C + 1], yt[:, k, g, 0:C], yt[:, k, g, :], start=False,
                                  stop=(q == PAIRS - 1 and k == 2 * q + 1 and g == G - 1))
                if q == PAIRS - 1:
                    last.then_inc(gram_mm, 1)

            keep_warm(WARM[0], pb_q)
            pe.wait_ge(bn_v, 1)
            pe.wait_ge(x_out, ITERS)
            combine(0)
            keep_warm(WARM[1], pb_q)
            pe.wait_ge(wabs_out, 2)
            for n in range(2):
                last = mm(pb_mean[:, n:n + 1], kst[:, K_ONES:K_ONES + P], wabs[n][:],
                          start=True, stop=True)
            last.then_inc(e_mm, 1)
            pe.wait_ge(taps_out, 1)
            for q in range(PAIRS):
                conv(0, q)
            keep_warm(WARM[2])
            pe.wait_ge(bn_v, 2)
            combine(1)
            keep_warm(WARM[3])
            pe.wait_ge(taps_out, 2)
            conv(1, 0)
            conv(1, 1)
            pe.wait_ge(lo_out, 4 * PAIRS - 2)
            conv_taps(1, 2, range(0, 5))
            pe.wait_ge(bn_v, 3)
            mm(pb_small[:, 0:1], kst[:, K_AVG:K_AVG + P], mv[2][:, 0:1], start=True, stop=True).then_inc(comb_mm, 1)
            conv_taps(1, 2, range(5, TAPS))
            mm(pb_gram[0:C, 0:C + 1], kst[0:C, K_ID:K_ID + C], kst[0:C, K_EPSN:K_EPSN + C + 1],
               start=True, stop=False)
            pe.wait_ge(lo_out, 4 * PAIRS)
            conv_taps(1, PAIRS - 1, range(0, 4))
            transposed(0)
            conv_taps(1, PAIRS - 1, range(4, TAPS))
            transposed(1)
            gram(0)
            transposed(2)
            gram(1)
            transposed(3)
            gram(2)
            gram(3)
            keep_warm(WARM[4])
            pe.wait_ge(cov_out, 2)
            mm(pb_small[:, R_COL:R_COL + Q * (Q + 1)], kst[0:C, K_REP:K_REP + P],
               cov_q[:].rearrange("p i r -> p (i r)"), start=True, stop=True).then_inc(rep_mm, 1)
            mm(pb_bias[:, 0:1], kst[0:C, K_AVG:K_AVG + P], cov[:, Q:Q + 1], start=True, stop=True).then_inc(sum_mm, 1)
            keep_warm(WARM[5])
            pe.wait_ge(fw_out, 1)
            pe.wait_ge(dmean_out, 1)
            mix_w = final_w[:].rearrange("p g q j -> p (g q j)")
            mm(pb_bias[:, 1:2], mix_w, dmean[:], start=True, stop=True).then_inc(bias_mm, 1)
            for q in range(PAIRS):
                mm(pb_out[q][:, 0:N], mix_w, yc[:, quarter(q)], start=True, stop=True).then_inc(fin_mm, 1)

        @block.vector
        def _(dve):
            ve = nc.vector
            steps = [0]

            def step(ins):
                ins.then_inc(dve_step, 1)
                steps[0] += 1
                dve.wait_ge(dve_step, steps[0])

            ve.memset(warm[:].bitcast(U32), 0).then_inc(warm_set, 1)
            dve.wait_ge(prm_in, 16)

            def power_of_two(n):
                t, col = bn_t[n], (P_BNG0, P_BNG1)[n]
                step(ve.tensor_reduce(t[:, 0:1], prm[:, col:col + 2], AX.X, ALU.max, apply_absolute_value=True))
                step(ve.tensor_scalar(t[:, 1:2], t[:, 0:1], 1e-30, 1.0 / FP16_ROOM, ALU.max, ALU.mult))
                step(ve.tensor_scalar(t[:, 2:3].bitcast(U32), t[:, 1:2].bitcast(U32), 0x7F800000, None,
                                      ALU.bitwise_and))
                ve.reciprocal(t[:, 3:4], t[:, 2:3]).then_inc(pow2_out, 1)
                dve.wait_ge(pow2_out, n + 1)
                step(ve.tensor_scalar(t[:, 4:6], prm[:, col:col + 2], t[:, 3:4], None, ALU.mult))

            def layer_constant():
                dve.wait_ge(wv0_set, 1)
                ve.tensor_scalar(const0[:], pb_e[:, P:P + 1], prm[:, P_BO:P_BO + 1],
                                 prm[:, P_GAMMA:P_GAMMA + 1], ALU.add, ALU.mult).then_inc(const0_set, 1)

            def weight_sum(n):
                dve.wait_ge(cw_in[n], 16)
                ve.tensor_reduce(wabs[n][:], cw[n][:], AX.XY, ALU.add,
                                 apply_absolute_value=True).then_inc(wabs_out, 1)

            def maxima(i, g):
                if i >= 2:
                    dve.wait_ge(shift_out, i - 1)
                dve.wait_ge(s_mm, 2 * i + g + 1)
                ve.tensor_reduce(negmax[:, i % 2, g * CH:(g + 1) * CH],
                                 pb_s[(2 * i + g) % 3][:].rearrange("p (t n) -> p t n", t=CH),
                                 AX.X, ALU.max, negate=True).then_inc(max_out, 1)

            def cut_first(i, o):
                m = (P_MQ1, P_MK1)[o]
                if i >= 1:
                    dve.wait_ge(rest_out, 2 * (i - 1) + o + 1)
                dve.wait_ge(qk_out, 2 * i + o + 1)
                ve.tensor_scalar(cut1[:, o], proj[:, i % 2, o], prm[:, m:m + 1], None,
                                 ALU.mult).then_inc(cut_out, 1)
                if i < DVE_RESTS:
                    dve.wait_ge(cut_out, 2 * i + o + 1)
                    ve.tensor_tensor(rest[:, o], proj[:, i % 2, o], cut1[:, o], ALU.subtract).then_inc(rest_out, 1)

            def cut_second(i, o):
                m = (P_MQ2, P_MK2)[o]
                dve.wait_ge(rest_out, 2 * i + o + 1)
                if i >= 1:
                    dve.wait_ge(parts_out, 2 * (i - 1) + o + 1)
                ve.tensor_scalar(cut2[:, o], rest[:, o], prm[:, m:m + 1], None, ALU.mult).then_inc(cut2_out, 1)

            def own_parts(i):
                dve.wait_ge(cut2_out, 2 * i + 2)
                ve.tensor_tensor(qk[:, i % DEPTH], rest[:], cut2[:], ALU.subtract).then_inc(parts_out, 2)

            def values_out(i):
                dve.wait_ge(v_mm, i + 1)
                if i >= 1:
                    dve.wait_ge(rows_out, i)
                if i >= 2:
                    dve.wait_ge(pv_mm, i - 1)
                ve.tensor_copy(vt[:, i % 2],
                               pb_v[:, 0:CH * P].rearrange("p (t c) -> p t c", t=CH)).then_inc(v_out, 1)

            def shifts(i):
                dve.wait_ge(ln_out, i + 1)
                if i >= 2:
                    dve.wait_ge(rows_mm, i - 1)
                p = shift_p[:, i % 2]
                ve.tensor_tensor(shift[:], negmax[:, i % 2, :], lntot[:, i % 2, :], ALU.subtract)
                step(ve.tensor_tensor(p[:, 0, :], negmax[:, i % 2, :], lntot[:, i % 2, :], ALU.subtract))
                ve.tensor_tensor(shift_r[:], shift[:], p[:, 0, :], ALU.subtract)
                step(ve.tensor_tensor(p[:, 1, :], shift[:], p[:, 0, :], ALU.subtract))
                ve.tensor_tensor(p[:, 2, :], shift_r[:], p[:, 1, :], ALU.subtract).then_inc(shift_out, 1)

            def add_shortcut(i):
                lay, b = divmod(i, PAIRS)
                dve.wait_ge(pv_mm, i + 1)
                const = const0[:] if lay == 0 else prm[:, P_BV1:P_BV1 + 1]
                cols = slice(b * N, (b + 1) * N)
                ve.scalar_tensor_tensor(xs[lay + 1][:, cols], mixed(i), const, xs[lay][:, cols],
                                        ALU.add, ALU.add).then_inc(x_out, 1)

            def statistics(b):
                dve.wait_ge(x_out, ITERS - PAIRS + b + 1)
                step(ve.bn_stats(stats[0][:, 6 * b:6 * b + 6], xs[LAYERS][:, b * N:(b + 1) * N]))

            for o in range(2):
                cut_first(0, o)
            for o in range(2):
                cut_second(0, o)
            layer_constant()
            own_parts(0)
            for o in range(2):
                cut_first(1, o)
            maxima(0, 0)
            maxima(0, 1)
            for o in range(2):
                cut_second(1, o)
            values_out(0)
            own_parts(1)
            shifts(0)
            cut_first(2, 0)
            maxima(1, 0)
            cut_first(2, 1)
            for i in range(ITERS - 2):
                maxima(i + 1, 1)
                cut_second(i + 2, 0)
                if i >= 1:
                    add_shortcut(i - 1)
                cut_second(i + 2, 1)
                values_out(i + 1)
                shifts(i + 1)
                if i + 3 < ITERS:
                    cut_first(i + 3, 0)
                    cut_first(i + 3, 1)
                maxima(i + 2, 0)
            maxima(ITERS - 1, 1)
            add_shortcut(ITERS - 3)
            values_out(ITERS - 1)
            statistics(0)
            shifts(ITERS - 1)
            statistics(1)
            for n in range(2):
                power_of_two(n)
            add_shortcut(ITERS - 2)
            statistics(2)
            ve.tensor_copy(tt[:, :, Q:2 * Q],
                           prm[:, P_W3:P_W3 + Q * Q].rearrange("p (i r) -> p i r", i=Q)).then_inc(w3_set, 1)
            add_shortcut(ITERS - 1)
            statistics(3)

            dve.wait_ge(kst_in, 16)

            def parts(n, q):
                if q == 0:
                    dve.wait_ge(bn_out, n + 1)
                    src = xs[LAYERS][:, quarter(0)] if n == 0 else z0[:]
                    if n == 1:
                        dve.wait_ge(z0_out, 1)
                    step(ve.tensor_scalar(act32[:, quarter(0)], src, bn_s[n][:], bn_b[n][:], ALU.mult, ALU.add))
                    step(ve.tensor_scalar(act32[:, quarter(0)], act32[:, quarter(0)], 0.0, None, ALU.max))
                else:
                    dve.wait_ge(act_out, n * (PAIRS - 1) + q)
                    ve.tensor_copy(padded(conv_in[n][0], lanes(0), q),
                                   img(act32[lanes(0), quarter(q)])).then_inc(hi0_out, 1)
                for g, hi_out in enumerate((hi0_out, hi1_out)):
                    dve.wait_ge(hi_out, n * PAIRS + q + 1)
                    ve.tensor_tensor(padded(conv_in[n][g], lanes(1 - g), q),
                                     img(act32[lanes(g), quarter(q)]), padded(conv_in[n][g], lanes(g), q),
                                     ALU.subtract).then_inc(lo_out, 1)

            for n in range(2):
                if n == 1:
                    dve.wait_ge(e_mm, 1)
                    step(ve.tensor_copy(emean[:], pb_mean[:, 0:2]))
                    step(ve.tensor_tensor(esq[:], emean[:, 0:1], emean[:, 0:1], ALU.mult))
                    step(ve.tensor_scalar(esq[:], esq[:], E_SQUARE_MIN, None, ALU.max))
                    step(ve.reciprocal(einv[:], esq[:]))
                    step(ve.tensor_scalar(eps1[:], einv[:], BN_EPS, None, ALU.mult))
                    for q in range(PAIRS):
                        dve.wait_ge(conv_mm, q + 1)
                        ve.bn_stats(stats[1][:, 6 * q:6 * q + 6], pb_conv[0][q][:, 0:N]).then_inc(stats_out, 1)
                        dve.wait_ge(stats_out, q + 1)
                ve.bn_aggr(mv[n][:], stats[n][:]).then_inc(bn_v, 1)
                if n == 0:
                    weight_sum(0)
                dve.wait_ge(comb_mm, n + 1)
                t = bn_t[n]
                step(ve.tensor_scalar(var[n][:], pb_small[:, 2:3], pb_small[:, 2:3],
                                      BN_EPS if n == 0 else eps1[:], ALU.mult, ALU.add))
                ve.tensor_tensor(var[n][:], pb_small[:, 1:2], var[n][:], ALU.add).then_inc(var_out, 1)
                if n == 0:
                    weight_sum(1)
                dve.wait_ge(rstd_out, n + 1)
                step(ve.tensor_tensor(bn_s[n][:], t[:, 4:5], rstd[n][:], ALU.mult))
                ve.scalar_tensor_tensor(bn_b[n][:], pb_small[:, 0:1], bn_s[n][:], t[:, 5:6], ALU.mult, ALU.subtract,
                                        reverse1=True).then_inc(bn_out, 1)
                dve.wait_ge(pads_set, 4)
                for q in range(PAIRS if n == 0 else PAIRS - 1):
                    parts(n, q)
            first = quarter(0)
            dve.wait_ge(conv_mm, PAIRS + 1)
            step(ve.scalar_tensor_tensor(yc[:, first], pb_conv[1][0][:, 0:N], emean[:, 1:2],
                                         xs[LAYERS][:, first], ALU.mult, ALU.add))
            step(ve.bn_stats(stats[2][:], yc[:, first]))
            ve.bn_aggr(mv[2][:], stats[2][:]).then_inc(bn_v, 1)
            parts(1, PAIRS - 1)
            dve.wait_ge(pre_out, 1)
            ve.tensor_scalar(yc[:, first], yc[:, first], npre[:], None, ALU.add).then_inc(yc_out, 1)
            for q in range(1, PAIRS):
                dve.wait_ge(conv_mm, PAIRS + q + 1)
                dve.wait_ge(xc_out, q)
                ve.scalar_tensor_tensor(yc[:, quarter(q)], pb_conv[1][q][:, 0:N], emean[:, 1:2],
                                        xc[:, quarter(q)], ALU.mult, ALU.add).then_inc(yc_out, 1)
            dve.wait_ge(gram_mm, 1)
            step(ve.tensor_tensor(gmask[:].rearrange("p q j -> p (q j)"), pb_gram[0:C, 0:C],
                                  kst[0:C, K_MASKJ:K_MASKJ + C], ALU.mult))
            ve.tensor_copy(cov[:, Q:Q + 1], pb_gram[0:C, C:C + 1]).then_inc(cov_out, 1)
            step(ve.tensor_reduce(cov[:, 0:Q], gmask[:], AX.X, ALU.add))
            dve.wait_ge(cov_out, 1)
            ve.tensor_tensor(cov_q[:], cov[:].unsqueeze(1).to_broadcast([C, Q, Q + 1]),
                             kst[0:C, K_HOT:K_HOT + Q].unsqueeze(2).to_broadcast([C, Q, Q + 1]),
                             ALU.mult).then_inc(cov_out, 1)
            dve.wait_ge(rep_mm, 1)
            dve.wait_ge(w3_set, 1)
            rep = pb_small[:, R_COL:R_COL + Q * (Q + 1)].rearrange("p (i r) -> p i r", i=Q)
            step(ve.tensor_copy(means[:], rep[:, :, Q]))
            step(ve.tensor_tensor(dd[:], means[:].unsqueeze(2).to_broadcast([P, Q, Q]),
                                  means[:].unsqueeze(1).to_broadcast([P, Q, Q]), ALU.mult))
            step(ve.tensor_tensor(tt[:, :, 0:Q], rep[:, :, 0:Q], dd[:], ALU.subtract))
            for j in range(Q - 1):
                left, rows = Q - 1 - j, 2 * Q - 1 - j
                ve.reciprocal(inv[:, j:j + 1], tt[:, j, j:j + 1]).then_inc(inv_out, 1)
                dve.wait_ge(inv_out, j + 1)
                col = tt[:, j:j + 1, j + 1:].to_broadcast([P, left, rows])
                lij = tt[:, j, j + 1:Q].unsqueeze(2).to_broadcast([P, left, rows])
                step(ve.scalar_tensor_tensor(upd[:, j + 1:, j + 1:], col, inv[:, j:j + 1], lij,
                                             ALU.mult, ALU.mult))
                step(ve.tensor_tensor(tt[:, j + 1:, j + 1:], tt[:, j + 1:, j + 1:], upd[:, j + 1:, j + 1:],
                                      ALU.subtract))
            end = Q - 1
            dve.wait_ge(own_out, end)
            ve.tensor_scalar(dpiv[:], tt[:, end, end:end + 1], hot[:, end:], own[:, end:end + 1],
                             ALU.mult, ALU.add).then_inc(piv_in, 1)
            step(ve.tensor_tensor(prod[:], tt[:, :, Q:2 * Q].rearrange("p i r -> p r i"),
                                  hot.unsqueeze(1).to_broadcast([P, Q, Q]), ALU.mult))
            step(ve.tensor_reduce(coef[:], prod[:], AX.X, ALU.add))
            dve.wait_ge(sum_mm, 1)
            ve.tensor_scalar(dmean[:], pb_bias[:, 0:1], -2.0 / NTOT, None,
                             ALU.mult).then_inc(dmean_out, 1)
            spread = coef[:].unsqueeze(1).unsqueeze(3).to_broadcast([P, G, Q, CJ])
            step(ve.tensor_tensor(placed[:], kst[:, K_MASKF:K_MASKF + P]
                                  .rearrange("p (g q j) -> p g q j", g=G, q=Q), spread, ALU.mult))
            dve.wait_ge(piv_out, 1)
            ve.tensor_scalar(final_w[:], placed[:], piv[:], None, ALU.mult).then_inc(fw_out, 1)
            dve.wait_ge(bias_mm, 1)
            ve.tensor_scalar(bias3[:], pb_bias[:, 1:2], prm[:, P_BIAS3:P_BIAS3 + 1], None,
                             ALU.add).then_inc(bias_out, 1)
            dve.wait_ge(bias_out, 1)
            for q in range(1, PAIRS, 2):
                dve.wait_ge(fin_mm, q + 1)
                ve.tensor_scalar(res[:, quarter(q)], pb_out[q][:, 0:N], bias3[:], None,
                                 ALU.add).then_inc(res_dve, 1)


def kernel(**inputs):
    import concourse.bacc as bacc
    from concourse.bass_utils import run_bass_kernel_spmd

    a = {name: np.asarray(v) for name, v in inputs.items()}

    def halves(m):
        return np.concatenate([m, m], axis=0)

    def diagonal(m, rows=C):
        out = np.zeros((P, P), m.dtype)
        out[0:m.shape[0], 0:m.shape[1]] = m
        out[rows:rows + m.shape[0], C:C + m.shape[1]] = m
        return out

    x = a["x"].reshape(G, PAIRS, C, N).transpose(0, 2, 1, 3).reshape(P, FREE)

    def groups(m):
        out = np.zeros(m.shape[:-1] + (C,), m.dtype)
        for n in range(len(PARTS)):
            out[..., n * CQ:(n + 1) * CQ] = m
        return out

    attn_w = np.concatenate([
        diagonal(groups(a["L0_conv_Wq"].T)), diagonal(groups(a["L0_conv_Wk"].T)),
        diagonal(a["L0_conv_Wv"], CV), diagonal(a["L0_conv_Wo"].T, CV),
        diagonal(groups(a["L1_conv_Wq"].T)), diagonal(groups(a["L1_conv_Wk"].T)),
        diagonal(a["L1_conv_Wv"].T)], axis=1)
    params = np.zeros((P, P_COLS), np.float32)
    for g in range(G):
        row = g * C
        for lay, (pq, pk) in enumerate(((P_BQ0, P_BK0), (P_BQ1, P_BK1))):
            params[row:row + C, pq] = groups(a[f"L{lay}_conv_bq"])
            params[row:row + C, pk] = groups(a[f"L{lay}_conv_bk"])
        for n, (part_q, part_k) in enumerate(PARTS):
            at = slice(row + n * CQ, row + (n + 1) * CQ)
            params[at, P_MQ1], params[at, P_MQ2] = part_q >= 1, part_q == 2
            params[at, P_MK1], params[at, P_MK2] = part_k >= 1, part_k == 2
        params[g * CV:(g + 1) * CV, P_BV0] = a["L0_conv_bv"]
    params[:, P_GAMMA] = a["L0_conv_gamma"][0]
    for col, name in ((P_BO, "L0_conv_bo"), (P_BV1, "L1_conv_bv"), (P_BNG0, "L2_conv_gamma0"),
                      (P_BNB0, "L2_conv_beta0"), (P_BNG1, "L2_conv_gamma1"), (P_BNB1, "L2_conv_beta1")):
        params[:, col] = halves(a[name])
    params[:, P_BIAS3] = halves(a["L3_conv_bias"].reshape(C))
    w3 = a["L3_conv_weight"].transpose(2, 1, 0).reshape(CJ, Q * Q)
    params[:, P_W3:P_W3 + Q * Q] = np.concatenate([w3] * (G * Q), axis=0)
    conv_w = [halves(a[f"L2_conv_w{n}"].reshape(C, C, TAPS).transpose(1, 2, 0).reshape(C, TAPS * C))
              for n in range(2)]

    nc = bacc.Bacc("TRN2", target_bir_lowering=False, num_devices=1)
    arrays = {"x_in": x, "attn_w": attn_w, "params": params, "consts": constants(),
              "select": selectors().reshape(SHIFTS, G * CH * P),
              "conv_w0": conv_w[0], "conv_w1": conv_w[1]}
    arrays = {name: np.ascontiguousarray(v) for name, v in arrays.items()}
    t = {name: nc.dram_tensor(name, v.shape, mybir.dt.from_np(v.dtype), kind="ExternalInput").ap()
         for name, v in arrays.items()}
    out = nc.dram_tensor("out", (P, FREE), F32, kind="ExternalOutput").ap()
    build(nc, t["x_in"], t["attn_w"], t["params"], t["consts"],
          t["select"].rearrange("p (n m) -> p n m", n=G * CH), [t["conv_w0"], t["conv_w1"]], out)
    r = run_bass_kernel_spmd(nc, [arrays], core_ids=[0])
    got = r.results[0]["out"]
    return got.reshape(G, C, PAIRS, N).transpose(0, 2, 1, 3).reshape(B, C, H, W)
```
